# Optimizing a Trainium2 kernel written in Bass

```python
import numpy as np
import jax
import jax.numpy as jnp

def _softmax(x, axis=-1):
    return jax.nn.softmax(x, axis=axis)

def _gelu(x):
    return jax.nn.gelu(x, approximate=True)

def _silu(x):
    return jax.nn.silu(x)

def _sigmoid(x):
    return jax.nn.sigmoid(x)

def _layernorm(x, axis=-1, eps=1e-05):
    m = jnp.mean(x, axis=axis, keepdims=True)
    v = jnp.var(x, axis=axis, keepdims=True)
    return (x - m) / jnp.sqrt(v + eps)

def _scatter_add(tgt, idx, src, axis=0):
    return tgt.at[idx].add(src)

def _segment_sum(src, seg, n):
    return jax.ops.segment_sum(src, seg, n)
kernel_name = 'mk_conv_attn_hybrid_d2_conv_nchw512_r4_6087c5'

def setup_inputs(seed: int=0):
    np.random.seed(seed)
    _w = jnp.asarray

    def _rec_inputs():
        import jax
        import jax.numpy as jnp
        _gk = jax.random.key(seed)
        x = -0.0003929 + 0.9999 * jax.random.normal(jax.random.fold_in(_gk, 1), (32, 128, 32, 32), jnp.float32)
        return x
    x = _rec_inputs()

    def _L0_conv_setup():
        import jax, jax.numpy as jnp
        import numpy as np
        GROUPS = 32
        EPS = 1e-05

        def _group_norm(x, w, b):
            B, C, H, W = x.shape
            xg = x.reshape(B, GROUPS, C // GROUPS, H, W)
            mean = xg.mean(axis=(2, 3, 4), keepdims=True)
            var = xg.var(axis=(2, 3, 4), keepdims=True)
            xg = (xg - mean) * jax.lax.rsqrt(var + EPS)
            return xg.reshape(B, C, H, W) * w[None, :, None, None] + b[None, :, None, None]
        key = jax.random.key(seed)
        ks = jax.random.split(key, 7)
        B, C, H, W = (32, 128, 32, 32)
        x = jax.random.normal(ks[0], (B, C, H, W), dtype=jnp.float32)
        gn_w = jnp.ones((C,), dtype=jnp.float32)
        gn_b = jnp.zeros((C,), dtype=jnp.float32)
        qkv_w = jax.random.normal(ks[1], (3 * C, C), dtype=jnp.float32) * C ** (-0.5)
        qkv_b = jax.random.normal(ks[2], (3 * C,), dtype=jnp.float32) * 0.02
        proj_w = jax.random.normal(ks[3], (C, C), dtype=jnp.float32) * C ** (-0.5)
        proj_b = jax.random.normal(ks[4], (C,), dtype=jnp.float32) * 0.02
        return {'x': x, 'gn_w': gn_w, 'gn_b': gn_b, 'qkv_w': qkv_w, 'qkv_b': qkv_b, 'proj_w': proj_w, 'proj_b': proj_b}
    _L0_conv_all = _L0_conv_setup()
    _L0_conv_in = {k: v for k, v in _L0_conv_all.items() if k in ('gn_w', 'gn_b', 'qkv_w', 'qkv_b', 'proj_w', 'proj_b')}
    del _L0_conv_all

    def _L1_attn_setup():
        import jax, jax.numpy as jnp
        import numpy as np
        D = 128
        H = 8
        W = 32
        HD = D // H
        EPS = 1e-05

        def _layernorm(x, g, b):
            mu = jnp.mean(x, axis=-1, keepdims=True)
            var = jnp.mean(jnp.square(x - mu), axis=-1, keepdims=True)
            return (x - mu) * jax.lax.rsqrt(var + EPS) * g + b
        key = jax.random.key(seed)
        ks = jax.random.split(key, 6)
        B, S = (4, 2048)
        src = jax.random.normal(ks[0], (B, S, D), jnp.float32)
        sc = 1.0 / np.sqrt(D)
        in_proj_w = jax.random.normal(ks[1], (3 * D, D), jnp.float32) * sc
        in_proj_b = jnp.zeros((3 * D,), jnp.float32)
        out_w = jax.random.normal(ks[2], (D, D), jnp.float32) * sc
        out_b = jnp.zeros((D,), jnp.float32)
        w1 = jax.random.normal(ks[3], (4 * D, D), jnp.float32) * sc
        b1 = jnp.zeros((4 * D,), jnp.float32)
        w2 = jax.random.normal(ks[4], (D, 4 * D), jnp.float32) * (1.0 / np.sqrt(4 * D))
        b2 = jnp.zeros((D,), jnp.float32)
        return {'src': src, 'in_proj_w': in_proj_w, 'in_proj_b': in_proj_b, 'out_w': out_w, 'out_b': out_b, 'ln1_g': jnp.ones((D,), jnp.float32), 'ln1_b': jnp.zeros((D,), jnp.float32), 'w1': w1, 'b1': b1, 'w2': w2, 'b2': b2, 'ln2_g': jnp.ones((D,), jnp.float32), 'ln2_b': jnp.zeros((D,), jnp.float32)}
    _L1_attn_all = _L1_attn_setup()
    _L1_attn_in = {k: v for k, v in _L1_attn_all.items() if k in ('in_proj_w', 'in_proj_b', 'out_w', 'out_b', 'ln1_g', 'ln1_b', 'w1', 'b1', 'w2', 'b2', 'ln2_g', 'ln2_b')}
    del _L1_attn_all

    def _L1_ffn_setup():
        import jax, jax.numpy as jnp
        import numpy as np
        E4M3_MAX = 448.0

        def qdq(x, scale, fp8_dtype, fmax):
            scaled = x / scale
            clipped = jnp.clip(scaled, -fmax, fmax)
            return clipped.astype(fp8_dtype).astype(x.dtype) * scale.astype(x.dtype)
        key = jax.random.key(seed)
        k1, k2, k3 = jax.random.split(key, 3)
        B, S, D, F = (8, 2048, 128, 128)
        x = jax.random.normal(k1, (B, S, D), jnp.float32)
        kernel = jax.random.normal(k2, (D, F), jnp.float32) * (1.0 / np.sqrt(D))
        bias = jax.random.normal(k3, (F,), jnp.float32) * 0.01
        return {'x': x, 'kernel': kernel, 'bias': bias, 'input_scale': jnp.ones((1,), jnp.float32), 'kernel_scale': jnp.ones((1,), jnp.float32), 'output_grad_scale': jnp.ones((1,), jnp.float32)}
    _L1_ffn_all = _L1_ffn_setup()
    _L1_ffn_in = {k: v for k, v in _L1_ffn_all.items() if k in ('kernel', 'bias', 'input_scale', 'kernel_scale', 'output_grad_scale')}
    del _L1_ffn_all
    return {'x': x, 'L0_conv_gn_w': _L0_conv_in['gn_w'], 'L0_conv_gn_b': _L0_conv_in['gn_b'], 'L0_conv_qkv_w': _L0_conv_in['qkv_w'], 'L0_conv_qkv_b': _L0_conv_in['qkv_b'], 'L0_conv_proj_w': _L0_conv_in['proj_w'], 'L0_conv_proj_b': _L0_conv_in['proj_b'], 'L1_attn_in_proj_w': _L1_attn_in['in_proj_w'], 'L1_attn_in_proj_b': _L1_attn_in['in_proj_b'], 'L1_attn_out_w': _L1_attn_in['out_w'], 'L1_attn_out_b': _L1_attn_in['out_b'], 'L1_attn_ln1_g': _L1_attn_in['ln1_g'], 'L1_attn_ln1_b': _L1_attn_in['ln1_b'], 'L1_attn_w1': _L1_attn_in['w1'], 'L1_attn_b1': _L1_attn_in['b1'], 'L1_attn_w2': _L1_attn_in['w2'], 'L1_attn_b2': _L1_attn_in['b2'], 'L1_attn_ln2_g': _L1_attn_in['ln2_g'], 'L1_attn_ln2_b': _L1_attn_in['ln2_b'], 'L1_ffn_kernel': _L1_ffn_in['kernel'], 'L1_ffn_bias': _L1_ffn_in['bias'], 'L1_ffn_input_scale': _L1_ffn_in['input_scale'], 'L1_ffn_kernel_scale': _L1_ffn_in['kernel_scale'], 'L1_ffn_output_grad_scale': _L1_ffn_in['output_grad_scale']}

def reference(x, L0_conv_gn_w, L0_conv_gn_b, L0_conv_qkv_w, L0_conv_qkv_b, L0_conv_proj_w, L0_conv_proj_b, L1_attn_in_proj_w, L1_attn_in_proj_b, L1_attn_out_w, L1_attn_out_b, L1_attn_ln1_g, L1_attn_ln1_b, L1_attn_w1, L1_attn_b1, L1_attn_w2, L1_attn_b2, L1_attn_ln2_g, L1_attn_ln2_b, L1_ffn_kernel, L1_ffn_bias, L1_ffn_input_scale, L1_ffn_kernel_scale, L1_ffn_output_grad_scale):
    import jax
    import jax.numpy as jnp

    def _L0_conv_ref(x, gn_w, gn_b, qkv_w, qkv_b, proj_w, proj_b):
        import jax, jax.numpy as jnp
        import numpy as np
        GROUPS = 32
        EPS = 1e-05

        def _group_norm(x, w, b):
            B, C, H, W = x.shape
            xg = x.reshape(B, GROUPS, C // GROUPS, H, W)
            mean = xg.mean(axis=(2, 3, 4), keepdims=True)
            var = xg.var(axis=(2, 3, 4), keepdims=True)
            xg = (xg - mean) * jax.lax.rsqrt(var + EPS)
            return xg.reshape(B, C, H, W) * w[None, :, None, None] + b[None, :, None, None]
        B, C, H, W = x.shape
        h = _group_norm(x, gn_w, gn_b).reshape(B, C, H * W)
        qkv = jnp.einsum('oc,bcn->bon', qkv_w, h) + qkv_b[None, :, None]
        q, k, v = jnp.split(qkv, 3, axis=1)
        scale = C ** (-0.5)
        attn = jax.nn.softmax(jnp.einsum('bcn,bcm->bnm', q, k) * scale, axis=-1)
        h = jnp.einsum('bcm,bnm->bcn', v, attn)
        h = jnp.einsum('oc,bcn->bon', proj_w, h) + proj_b[None, :, None]
        return x + h.reshape(B, C, H, W)

    def _L1_attn_ref(src, in_proj_w, in_proj_b, out_w, out_b, ln1_g, ln1_b, w1, b1, w2, b2, ln2_g, ln2_b):
        import jax, jax.numpy as jnp
        import numpy as np
        D = 128
        H = 8
        W = 32
        HD = D // H
        EPS = 1e-05

        def _layernorm(x, g, b):
            mu = jnp.mean(x, axis=-1, keepdims=True)
            var = jnp.mean(jnp.square(x - mu), axis=-1, keepdims=True)
            return (x - mu) * jax.lax.rsqrt(var + EPS) * g + b
        B, S, _ = src.shape
        nW = S // W
        x = src.reshape(B, nW, W, D)
        qkv = jnp.einsum('bnwd,ed->bnwe', x, in_proj_w) + in_proj_b
        q, k, v = jnp.split(qkv, 3, axis=-1)
        q = q.reshape(B, nW, W, H, HD)
        k = k.reshape(B, nW, W, H, HD)
        v = v.reshape(B, nW, W, H, HD)
        scores = jnp.einsum('bnqhd,bnkhd->bnhqk', q, k) / np.sqrt(HD)
        probs = jax.nn.softmax(scores, axis=-1)
        attn = jnp.einsum('bnhqk,bnkhd->bnqhd', probs, v).reshape(B, nW, W, D)
        attn = jnp.einsum('bnwd,ed->bnwe', attn, out_w) + out_b
        x = _layernorm(x + attn, ln1_g, ln1_b)
        ff = jnp.einsum('bnwf,df->bnwd', jax.nn.relu(jnp.einsum('bnwd,fd->bnwf', x, w1) + b1), w2) + b2
        x = _layernorm(x + ff, ln2_g, ln2_b)
        return x.reshape(B, S, D)

    def _L1_ffn_ref(x, kernel, bias, input_scale, kernel_scale, output_grad_scale):
        import jax, jax.numpy as jnp
        import numpy as np
        E4M3_MAX = 448.0

        def qdq(x, scale, fp8_dtype, fmax):
            scaled = x / scale
            clipped = jnp.clip(scaled, -fmax, fmax)
            return clipped.astype(fp8_dtype).astype(x.dtype) * scale.astype(x.dtype)
        B, S, D = x.shape
        inp_mat = x.reshape(-1, D)
        inp_q = qdq(inp_mat, input_scale, jnp.float8_e4m3fn, E4M3_MAX)
        ker_q = qdq(kernel, kernel_scale, jnp.float8_e4m3fn, E4M3_MAX)
        out = inp_q @ ker_q
        b = bias.astype(jnp.bfloat16).astype(jnp.float32)
        out = out + b
        return out.reshape(B, S, out.shape[-1])

    def _gn(v, G=32, eps=1e-05):
        B_, C_, H_, W_ = v.shape
        g = v.reshape(B_, G, C_ // G, H_, W_)
        m = jnp.mean(g, axis=(2, 3, 4), keepdims=True)
        s = jnp.var(g, axis=(2, 3, 4), keepdims=True)
        return ((g - m) / jnp.sqrt(s + eps)).reshape(v.shape)

    def _ln_c(v, eps=1e-06):
        m = jnp.mean(v, axis=1, keepdims=True)
        s = jnp.var(v, axis=1, keepdims=True)
        return (v - m) / jnp.sqrt(s + eps)

    def _ln_t(v, eps=1e-05):
        m = jnp.mean(v, axis=-1, keepdims=True)
        s = jnp.var(v, axis=-1, keepdims=True)
        return (v - m) / jnp.sqrt(s + eps)

    def _to_tokens(v):
        B_, C_, H_, W_ = v.shape
        return v.reshape(B_, C_, H_ * W_).transpose(0, 2, 1)

    def _from_tokens(t, like):
        B_, C_, H_, W_ = like.shape
        return t.transpose(0, 2, 1).reshape(B_, C_, H_, W_)
    x = _L0_conv_ref(x, L0_conv_gn_w, L0_conv_gn_b, L0_conv_qkv_w, L0_conv_qkv_b, L0_conv_proj_w, L0_conv_proj_b)
    t = _to_tokens(x)
    t = t + _L1_attn_ref(_ln_t(t), L1_attn_in_proj_w, L1_attn_in_proj_b, L1_attn_out_w, L1_attn_out_b, L1_attn_ln1_g, L1_attn_ln1_b, L1_attn_w1, L1_attn_b1, L1_attn_w2, L1_attn_b2, L1_attn_ln2_g, L1_attn_ln2_b)
    t = t + _L1_ffn_ref(_ln_t(t), L1_ffn_kernel, L1_ffn_bias, L1_ffn_input_scale, L1_ffn_kernel_scale, L1_ffn_output_grad_scale)
    x = _from_tokens(t, x)
    return x

_drawn_inputs = setup_inputs


def setup_inputs(seed=0):
    import zlib

    import numpy as np

    out = dict(_drawn_inputs(seed))
    spreads = {'L0_conv_gn_w': (1.0, 0.2),
     'L0_conv_gn_b': (0.0, 0.1),
     'L1_attn_in_proj_b': (0.0, 0.1),
     'L1_attn_out_b': (0.0, 0.1),
     'L1_attn_ln1_g': (1.0, 0.2),
     'L1_attn_ln1_b': (0.0, 0.1),
     'L1_attn_b1': (0.0, 0.1),
     'L1_attn_b2': (0.0, 0.1),
     'L1_attn_ln2_g': (1.0, 0.2),
     'L1_attn_ln2_b': (0.0, 0.1)}
    factors = {'L1_ffn_bias': 8.0}
    for name, (base, spread) in spreads.items():
        noise = np.random.default_rng([zlib.crc32(name.encode()), seed]).standard_normal(out[name].shape)
        drawn = base * np.exp(spread * noise) if base else spread * noise
        out[name] = jnp.asarray(drawn.astype(out[name].dtype))
    for name, factor in factors.items():
        out[name] = (out[name] * factor).astype(out[name].dtype)
    return out
```

```python
from contextlib import ExitStack

import concourse.bass as bass
import numpy as np
from concourse import mybir

F32 = mybir.dt.float32
F16 = mybir.dt.float16
BF16 = mybir.dt.bfloat16
I32 = mybir.dt.int32
ALU = mybir.AluOpType
ACT = mybir.ActivationFunctionType
X = mybir.AxisListType.X

IMAGES, C, N = 32, 128, 1024
P = 128
HALF = 512
HT = HALF // P
MT = N // P
GROUP = C // 32
HEADS, HD, WIN = 8, 16, 32
FF = 4 * C
FT = FF // P
PVW = C + 1
SLOTS = 24
FIRST_ST = 8
PV_LAG = 2
PRING = 4
EPS = 1e-5
E4M3_MAX = 448.0
EXP_MASK = 0x7F800000
E4M3_MIN_NORMAL = 2.0 ** -6
ROUND_3_BITS = 1.5 * 2.0 ** 20

STEPS = [("ln_in", 0), ("norm_in", 1), ("turn_in", 2), ("q", 3), ("k", 3), ("v", 4), ("score0", 5),
         ("prob0", 6), ("score1", 6), ("place0", 7), ("prob1", 7), ("place1", 8), ("pv0", 10), ("pv1", 11),
         ("out", 12), ("norm_mid", 13), ("turn_mid", 14), ("up0", 15), ("up1", 15), ("up2", 16), ("up3", 16),
         ("down", 17), ("norm_out", 18), ("ln_q", 19), ("quant", 20), ("turn_q", 21), ("ffn", 22)]


def schedule():
    slots = [[] for _ in range(SLOTS)]

    def put(slot, name, index):
        slots[slot % SLOTS].append((name, index, slot // SLOTS))

    for c in range(2):
        put(0, "qg", c)
        put(0, "kg", c)
        put(3, "turn_x", c)
        put(2, "vg", c)
    for c in range(2 * MT):
        put(FIRST_ST + c, "st", c)
        put(FIRST_ST + c + PV_LAG, "pv", c)
    chunk = 0
    for slot, count in zip(range(1, 8), (1, 2, 2, 3, 3, 3, 2)):
        for _ in range(count):
            put(slot, "max", chunk)
            chunk += 1
            if chunk in (MT, 2 * MT):
                put(slot + (chunk == MT), "shift", chunk // MT - 1)
    for h in range(2):
        for name, offset in STEPS:
            put(FIRST_ST + MT * (h + 1) + PV_LAG - 1 + offset, name, h)
    put(14, "load_x", 0)
    put(17, "gn0", 0)
    put(18, "gn1", 0)
    put(20, "gn2", 0)
    return slots


SCHEDULE = schedule()
NEXT = ("load_x", "gn0", "gn1", "gn2")

GLOBAL_BANKS, LAYER_BANKS, PV_BANKS = (0, 1, 2), (3, 4, 5), (6, 7)
GLOBAL_USES = ("qg", "kg", "vg", "turn_x", "max", "shift", "st", "gn1", "gn2")
LAYER_USES = ("turn_in", "q", "k", "v", "score0", "score1", "pv0", "out", "turn_mid", "up0", "up1",
              "up2", "up3", "down", "turn_q", "ffn")

RELEASE = {
    "qg": ("qg_lo", 2, False), "kg": ("kg_lo", 2, False), "vg": ("vg_lo", 2, False),
    "turn_x": ("xt_made", 2, False), "max": ("max_out", 2 * MT, False), "shift": ("shift_made", 2, False),
    "st": ("p_made", 2 * MT, False), "gn1": ("gn_mean", 1, False), "gn2": ("gn_veps", 1, False),
    "turn_in": ("x_lo", 1, True), "q": ("q_lo", 1, True), "k": ("k_lo", 1, True), "v": ("v_lo", 1, True),
    "score0": ("sub_made", 2, True), "score1": ("sub_made", 2, True), "pv0": ("o_lo", 1, True),
    "out": ("y1_made", 1, True), "turn_mid": ("m_lo", 1, True), "up0": ("hid_made", FT, True),
    "up1": ("hid_made", FT, True), "up2": ("hid_made", FT, True), "up3": ("hid_made", FT, True),
    "down": ("y2_made", 1, True), "turn_q": ("qt_made", 1, True), "ffn": ("o_made", 1, True),
}


def bank_table():
    bank, turn = {}, {GLOBAL_USES: 0, LAYER_USES: 0}
    for slot in SCHEDULE:
        for name, index, _ in slot:
            for uses, banks in ((GLOBAL_USES, GLOBAL_BANKS), (LAYER_USES, LAYER_BANKS)):
                if name in uses:
                    bank[name, index] = banks[turn[uses] % 3]
                    turn[uses] += 1
    return bank


BANK = bank_table()


def steps_of(new, old, nxt):
    for slot in SCHEDULE:
        for name, index, lag in slot:
            if (name in NEXT and nxt) or (name not in NEXT and (old if lag else new)):
                yield name, index, -1 if lag else 1 if name in NEXT else 0


def tenants(images):
    holder, table = {}, {}

    def iteration(kind, i, steps):
        for name, index, off in steps:
            if (name, index) in BANK:
                b, img = BANK[name, index], i + off
                if b in holder:
                    pname, pindex, pimg = holder[b]
                    table[kind, name, index] = (pname, pindex, img - pimg)
                holder[b] = (name, index, img)

    iteration("prologue", -1, [("gn1", 0, 1), ("gn2", 0, 1)])
    iteration("first", 0, steps_of(True, False, True))
    iteration("second", 1, steps_of(True, True, True))
    for i in range(2, images - 1):
        iteration("steady", i, steps_of(True, True, True))
    iteration("last", images - 1, steps_of(True, True, False))
    iteration("tail", images, steps_of(False, True, False))
    return table


def build(nc, a, out, images=IMAGES):
    ctx = ExitStack()
    with ctx:
        def sb(name, shape, dt=F32):
            return ctx.enter_context(nc.sbuf_tensor(name, shape, dt))

        def sem(name):
            return ctx.enter_context(nc.semaphore(name))

        QG, KG, VG, PROJ, Q, K, V, OUT, PVG = range(9)
        wh, wl = sb("wh", [P, 9, P], F16), sb("wl", [P, 9, P], BF16)
        w1h, w1l = sb("w1h", [P, FF], F16), sb("w1l", [P, FF], BF16)
        w2h, w2l = sb("w2h", [P, FT, P], F16), sb("w2l", [P, FT, P], BF16)
        kh, kl = sb("kh", [P, P], F16), sb("kl", [P, P], BF16)
        cols = sb("cols", [P, 26])
        (QGB, KGB, VGB, PROJB, GNW, GNB, QB, KB, VB, LN1B, FFNB, B1) = range(12)
        B1F, BFB, LN1G, S_IN, S_K, R_IN, R_K, S_BOTH = 15, 19, 20, 21, 22, 23, 24, 25

        def col(c):
            return cols[:, c:c + 1]

        spare = sb("spare", [P, 1])
        ffnb16 = sb("ffnb16", [P, 1], BF16)
        BO, RG1, RB1, RB2, RG2, RBL2, PROJR = range(7)
        rows = sb("rows", [P, 7, P])

        def row(r):
            return rows[:, r:r + 1, :].to_broadcast([P, HT, P])

        identf, identh = sb("identf", [P, P]), sb("identh", [P, P], BF16)
        group_mean = sb("group_mean", [P, P])
        sel = sb("sel", [2 * HT, HT, P])
        minus1 = sb("minus1", [P, P], BF16)
        halfpow = sb("halfpow", [P, HT])
        ones = sb("ones", [P, P])
        vb_full = sb("vb_full", [P, 2, P])

        x_sb = sb("x_sb", [P, N])
        xt = sb("xt", [P, 2, HT, P])
        gst, gmv = sb("gst", [P, 2, 6]), sb("gmv", [P, 2])
        GMEAN, GDIFF, GVAR, GEPS, GRSTD, GSCALE, GNEG, GBIAS = range(8)
        gtmp = sb("gtmp", [P, 8])

        def gt(c):
            return gtmp[:, c:c + 1]

        h32 = sb("h32", [P, N])
        hh, hl = sb("hh", [P, N], F16), sb("hl", [P, N], F16)
        qgh, qgl = sb("qgh", [P, N], F16), sb("qgl", [P, N], F16)
        kgh, kgl = sb("kgh", [P, N], F16), sb("kgl", [P, N], F16)
        vgh, vgl = sb("vgh", [P, MT, PVW], F16), sb("vgl", [P, MT, P], F16)
        cm = sb("cm", [P, MT, 2])
        cmax = sb("cmax", [P, HT])
        chi = sb("chi", [P, HT], BF16)
        cparts = sb("cparts", [P, P])
        shift = sb("shift", [P, 2, HT, P], BF16)
        p32 = sb("p32", [P, PRING, HALF])
        ph, pl = sb("ph", [P, PRING, HALF], F16), sb("pl", [P, PRING, HALF], F16)
        rsum = sb("rsum", [P, 2, 2])

        t = sb("t", [P, 2, HT, P])
        stats, mv = sb("stats", [P, 2, HT, 6]), sb("mv", [P, 2, HT, 2])
        veps, rstd = sb("veps", [P, 2, HT]), sb("rstd", [P, 2, HT])
        xh, xl = sb("xh", [P, 2, HALF], F16), sb("xl", [P, 2, HALF], F16)
        qh, ql = sb("qh", [P, 2, HALF], F16), sb("ql", [P, 2, HALF], F16)
        kk = sb("kk", [P, 2, 2, HALF], F16)
        kbd = sb("kbd", [P, 2, HEADS, 2, HALF], F16)
        vh, vl = sb("vh", [P, 2, 2, HT, P], F16), sb("vl", [P, 2, 2, HT, P], F16)
        smax, ssum, srec = sb("smax", [P, 2, 16]), sb("ssum", [P, 2, 16]), sb("srec", [P, 2, 16])
        e, et = sb("e", [P, 2, HALF]), sb("et", [P, 2, HALF])
        pt = sb("pt", [P, 2, 2, 2, HALF], F16)
        ptbd = sb("ptbd", [P, 2, 2, HT, 4, HALF // 2], F16)
        oh, ol = sb("oh", [P, 2, HALF], F16), sb("ol", [P, 2, HALF], F16)
        y = sb("y", [P, 2, HT, P])
        res = sb("res", [P, 2, HT, P])
        hid = sb("hid", [P, 2, HALF])
        fh, fl = sb("fh", [P, FT, HALF], F16), sb("fl", [P, FT, HALF], F16)
        z, expo = sb("z", [P, HALF]), sb("expo", [P, HALF])
        qz = sb("qz", [P, 2, HT, P], BF16)
        qt = sb("qt", [P, 2, HALF], BF16)
        o_sb = sb("o_sb", [P, 2, HALF])
        wraw = xt[:].rearrange("p a b c -> p (a b) c")
        w1raw, w2raw, kraw = e[:, 0, :], e[:, 1, :].rearrange("p (a b) -> p a b", b=P), et[:, 0, 0:P]
        ps = ctx.enter_context(nc.psum_tensor("ps", [P, 8, HALF], F32))

        def bank(name, index):
            return ps[:, BANK[name, index], :]

        def tiles(ap):
            return ap.rearrange("p (a b) -> p a b", b=P)

        s = {n: sem(n) for n in """weights_in const_made const_mask setup_dve setup_mm
            x_in gn_stats gn_mv gn_mm gn_mean gn_diff gn_var gn_veps gn_pow gn_scale gn_neg gn_coef h32_made h_hi h_lo
            qg_mm kg_mm vg_mm turn_x_mm qg_hi kg_hi vg_hi qg_lo kg_lo vg_lo xt_made
            max_mm max_out cmax_made chi_made cparts_made shift_turned shift_made
            st_mm p_made p_hi p_lo pv_mm rsum_made t_made
            xr_made turn_in_mm turn_mid_mm x_hi x_lo q_mm k_mm v_mm
            q_hi q_lo k_hi k_lo v_hi v_lo score_mm smax_made sub_made exp_made ssum_made srec_made prob_made
            et_made pt_hi pt_lo pv_win_mm o_hi o_lo out_mm y1_made r1a_made r1_made m_hi m_lo
            up_mm hid_made hid_hi hid_lo down_mm y2_made t2a_made t2b_made t2_made scaled z_made clipped
            expo_made expo_low u_made rounded qz_made turn_q_mm qt_made ffn_mm o_made""".split()}
        s.update({n: sem(n) for h in range(2) for n in (f"keys_in{h}", f"probs_in{h}0", f"probs_in{h}1", f"stored{h}")})
        s.update({f"{n}{k}": sem(f"{n}{k}") for k in range(4) for n in ("ln_stats", "ln_mv", "ln_veps", "ln_pow", "norm_made")})

        def upto(unit, k=1, per=1, step=1):
            return (unit * per + k) * step

        def due(value):
            return not isinstance(value, int) or value > 0

        before = tenants(images)
        block = ctx.enter_context(nc.Block())

        def run(engine, table, prologue):
            prologue()

            def iteration(kind, i, new, old, nxt):
                for name, index, off in steps_of(new, old, nxt):
                    if name in table:
                        table[name](kind, i + off, index)

            iteration("first", 0, True, False, True)
            iteration("second", 1, True, True, True)
            with engine.Fori(2, images - 1) as i:
                iteration("steady", i, True, True, True)
            iteration("last", images - 1, True, True, False)
            iteration("tail", images, False, True, False)

        @block.sync
        def _(sp):
            def load(dst, src):
                sp.dma_start(dst, src).then_inc(s["weights_in"], 16)

            def prologue():
                sp.dma_start(x_sb[:, :], a["x"][0]).then_inc(s["x_in"], 16)
                load(wraw[:, QG:QG + 2, :].rearrange("p a b -> p (a b)"), a["qkv_w_t"][:, 0:2 * P])
                load(wraw[:, VG, :], a["v_w"])
                load(wraw[:, PROJ, :], a["proj_w_t"])
                load(wraw[:, Q:Q + 3, :].rearrange("p a b -> p (a b)"), a["in_w_t"])
                load(wraw[:, OUT, :], a["out_w_t"])
                load(w1raw, a["w1_t"])
                load(w2raw, a["w2_t"].rearrange("(t p) d -> p t d", p=P))
                load(kraw, a["kernel"])
                with nc.allow_non_contiguous_dma("short vectors, once"):
                    for at, width, name in ((QGB, 3, "qkv_b"), (PROJB, 1, "proj_b"), (GNW, 1, "gn_w"), (GNB, 1, "gn_b"),
                                            (QB, 3, "in_b"), (LN1B, 1, "ln1_b"), (FFNB, 1, "ffn_b"), (B1, FT, "b1"),
                                            (LN1G, 1, "ln1_g")):
                        load(cols[:, at:at + width], a[name].rearrange("(t p) -> p t", p=P))
                    load(col(S_IN), a["s_in"].partition_broadcast(P))
                    load(col(S_K), a["s_k"].partition_broadcast(P))
                for at, name in ((BO, "out_b"), (RG1, "ln1_g"), (RB1, "ln1_b"), (RB2, "b2"), (RG2, "ln2_g"),
                                 (RBL2, "ln2_b"), (PROJR, "proj_b")):
                    load(rows[:, at, :], a[name].partition_broadcast(P))

            def place_keys(kind, img, h):
                sp.wait_ge(s["k_hi"], upto(2 * img + h))
                sp.wait_ge(s["k_lo"], upto(2 * img + h))
                for head in range(HEADS):
                    mine = slice(HD * head, HD * (head + 1))
                    sp.dma_start(kbd[mine, h, head, :, :], kk[mine, h, :, :]).then_inc(s[f"keys_in{h}"], 16)

            def place_probs(pair):
                def step(kind, img, h):
                    sp.wait_ge(s["pt_hi"], upto(2 * img + h, pair + 1, per=2))
                    sp.wait_ge(s["pt_lo"], upto(2 * img + h, pair + 1, per=2))
                    for w in range(4):
                        mine = slice(WIN * w, WIN * (w + 1))
                        for part in range(2):
                            sp.dma_start(ptbd[mine, h, part, 2 * pair:2 * pair + 2, w, :],
                                         pt[mine, h, pair, part, :].rearrange("p (a b) -> p a b", a=2)).then_inc(s[f"probs_in{h}{pair}"], 16)
                return step

            run(sp, {"k": place_keys, "place0": place_probs(0), "place1": place_probs(1)}, prologue)
            for h in range(2):
                sp.wait_ge(s[f"stored{h}"], 16 * images)

        @block.gpsimd
        def _(pool):
            g = nc.gpsimd

            def prologue():
                for tile, value in ((identf, 0.0), (identh, 0.0), (sel, 0.0), (group_mean, 1.0 / GROUP), (halfpow, -0.5)):
                    g.memset(tile[:], value).then_inc(s["const_made"], 1)
                pool.wait_ge(s["const_made"], 5)
                for tile in (identf, identh):
                    g.affine_select(out=tile[:], in_=tile[:], compare_op=ALU.not_equal, fill=1.0, base=0,
                                    pattern=[[-1, P]], channel_multiplier=1).then_inc(s["const_mask"], 1)
                gm = group_mean[:].rearrange("p (a b) -> p a b", b=GROUP)
                g.affine_select(out=gm, in_=gm, compare_op=ALU.is_ge, fill=0.0, base=0,
                                pattern=[[-GROUP, P // GROUP], [0, GROUP]], channel_multiplier=1).then_inc(s["const_mask"], 1)
                g.affine_select(out=sel[:], in_=sel[:], compare_op=ALU.not_equal, fill=1.0, base=0,
                                pattern=[[-1, HT], [0, P]], channel_multiplier=1).then_inc(s["const_mask"], 1)
                pool.wait_ge(s["const_mask"], 4)
                g.affine_select(out=gm, in_=gm, compare_op=ALU.is_ge, fill=0.0, base=GROUP - 1,
                                pattern=[[GROUP, P // GROUP], [0, GROUP]], channel_multiplier=-1).then_inc(s["const_mask"], 1)
                g.affine_select(out=sel[:], in_=sel[:], compare_op=ALU.not_equal, fill=1.0, base=-HT,
                                pattern=[[-1, HT], [0, P]], channel_multiplier=1).then_inc(s["const_mask"], 1)
                for tile, value in ((cparts, 0.0), (minus1, -1.0), (vgh, 1.0), (ones, 1.0), (shift, 0.0)):
                    g.memset(tile[:], value).then_inc(s["const_made"], 1)
                gn2(None, 0, 0)
                for tile in (vh, vl, kbd, ptbd):
                    g.memset(tile[:], 0.0).then_inc(s["const_made"], 1)

            def gn2(kind, img, _):
                pool.wait_ge(s["gn_veps"], upto(img))
                g.tensor_tensor(gt(GRSTD), gt(GEPS), halfpow[:, 0:1], ALU.pow).then_inc(s["gn_pow"], 1)
                pool.wait_ge(s["h32_made"], upto(img))
                pool.wait_ge(s["h_hi"], upto(img))
                if due(value := upto(img - 1, 2, per=2)):
                    pool.wait_ge(s["vg_mm"], value)
                g.tensor_tensor(hl[:], h32[:], hh[:], ALU.subtract).then_inc(s["h_lo"], 1)

            def st(kind, img, c):
                pool.wait_ge(s["p_hi"], upto(img, c + 1, per=2 * MT))
                if due(value := upto(img, c + 1 - PRING, per=2 * MT)):
                    pool.wait_ge(s["pv_mm"], value)
                g.tensor_tensor(pl[:, c % PRING, :], p32[:, c % PRING, :], ph[:, c % PRING, :],
                                ALU.subtract).then_inc(s["p_lo"], 1)

            def power(n, k, h):
                pool.wait_ge(s[f"ln_veps{k}"], upto(n))
                g.tensor_tensor(rstd[:, h, :], veps[:, h, :], halfpow[:], ALU.pow).then_inc(s[f"ln_pow{k}"], 1)

            def power_step(k):
                def step(kind, img, h):
                    power(2 * img + h, k, h)
                return step

            def norm_in(kind, img, h):
                pool.wait_ge(s["norm_made0"], upto(2 * img + h))
                g.tensor_tensor(res[:, h], y[:, h], row(BO), ALU.add).then_inc(s["xr_made"], 1)

            def place_lo(pair):
                def step(kind, img, h):
                    n = 2 * img + h
                    pool.wait_ge(s["pt_hi"], upto(n, pair + 1, per=2))
                    if due(value := upto(img - 1, 8, per=8, step=16)):
                        pool.wait_ge(s[f"probs_in{h}{pair}"], value)
                    g.tensor_tensor(pt[:, h, pair, 1, :], et[:, h, :], pt[:, h, pair, 0, :],
                                    ALU.subtract).then_inc(s["pt_lo"], 1)
                return step

            def norm_mid(kind, img, h):
                n = 2 * img + h
                pool.wait_ge(s["norm_made1"], upto(n))
                g.tensor_tensor(res[:, h], y[:, h], row(RG1), ALU.mult).then_inc(s["r1a_made"], 1)
                pool.wait_ge(s["r1a_made"], upto(n))
                g.tensor_tensor(res[:, h], res[:, h], row(RB1), ALU.add).then_inc(s["r1_made"], 1)

            def up(f):
                def step(kind, img, h):
                    n = 2 * img + h
                    pool.wait_ge(s["hid_hi"], upto(n, f + 1, per=FT))
                    if due(value := upto(n - 1)):
                        pool.wait_ge(s["down_mm"], value)
                    g.tensor_tensor(fl[:, f, :], hid[:, f % 2, :], fh[:, f, :], ALU.subtract).then_inc(s["hid_lo"], 1)
                return step

            def norm_out(kind, img, h):
                n = 2 * img + h
                g.tensor_tensor(t[:, h], t[:, h], row(RBL2), ALU.add).then_inc(s["t2b_made"], 1)
                pool.wait_ge(s["norm_made2"], upto(n))
                g.tensor_tensor(y[:, h], y[:, h], row(RG2), ALU.mult).then_inc(s["t2a_made"], 1)
                pool.wait_ge(s["t2a_made"], upto(n))
                pool.wait_ge(s["t2b_made"], upto(n))
                g.tensor_tensor(t[:, h], t[:, h], y[:, h], ALU.add).then_inc(s["t2_made"], 1)

            run(pool, {"gn2": gn2, "st": st, "ln_in": power_step(0), "norm_in": norm_in, "place0": place_lo(0),
                       "place1": place_lo(1), "out": power_step(1), "norm_mid": norm_mid, "up0": up(0), "up1": up(1),
                       "up2": up(2), "up3": up(3), "down": power_step(2), "norm_out": norm_out,
                       "ln_q": power_step(3)}, prologue)

        @block.scalar
        def _(act):
            sc = nc.scalar

            def prologue():
                gn2(None, 0, 0)

            def gn2(kind, img, _):
                act.wait_ge(s["gn_coef"], upto(img))
                act.wait_ge(s["x_in"], upto(img, step=16))
                if due(value := upto(img - 1, 2, per=2)):
                    act.wait_ge(s["vg_mm"], value)
                sc.activation(hh[:], x_sb[:], ACT.Identity, bias=gt(GBIAS), scale=gt(GSCALE)).then_inc(s["h_hi"], 1)

            def load_x(kind, img, _):
                if due(value := upto(img - 1, 2, per=2)):
                    act.wait_ge(s["turn_x_mm"], value)
                if due(value := upto(img - 1)):
                    act.wait_ge(s["h_hi"], value)
                if due(value := upto(img - 1)):
                    act.wait_ge(s["h32_made"], value)
                act.dma_start(x_sb[:, :], a["x"][img]).then_inc(s["x_in"], 16)

            def global_hi(name, dst, bias):
                def step(kind, img, c):
                    act.wait_ge(s[name + "_mm"], upto(img, c + 1, per=2))
                    sc.activation(dst[:, HALF * c:HALF * (c + 1)], bank(name, c), ACT.Identity,
                                  bias=col(bias)).then_inc(s[name + "_hi"], 1)
                return step

            def vg(kind, img, c):
                act.wait_ge(s["vg_mm"], upto(img, c + 1, per=2))
                if kind == "first" and c == 0:
                    act.wait_ge(s["const_made"], 10)
                sc.activation(vgh[:, HT * c:HT * (c + 1), 0:C], tiles(bank("vg", c)), ACT.Copy).then_inc(s["vg_hi"], 1)

            def st(kind, img, c):
                act.wait_ge(s["st_mm"], upto(img, c + 1, per=2 * MT))
                if due(value := upto(img, c + 1 - PRING, per=2 * MT)):
                    act.wait_ge(s["p_lo"], value)
                sc.activation(p32[:, c % PRING, :], bank("st", c), ACT.Exp, scale=C ** -0.5).then_inc(s["p_made"], 1)

            def turned_hi(name, signal):
                def step(kind, img, h):
                    n = 2 * img + h
                    act.wait_ge(s[name + "_mm"], upto(n))
                    sc.activation(xh[:, h, :], bank(name, h), ACT.Copy).then_inc(s[signal], 1)
                return step

            def q(kind, img, h):
                act.wait_ge(s["q_mm"], upto(2 * img + h))
                sc.activation(qh[:, h, :], bank("q", h), ACT.Identity, bias=col(QB)).then_inc(s["q_hi"], 1)

            def k(kind, img, h):
                n = 2 * img + h
                act.wait_ge(s["k_mm"], upto(n))
                if due(value := upto(img - 1, HEADS, per=HEADS, step=16)):
                    act.wait_ge(s[f"keys_in{h}"], value)
                sc.activation(kk[:, h, 0, :], bank("k", h), ACT.Identity, bias=col(KB)).then_inc(s["k_hi"], 1)

            def v(kind, img, h):
                n = 2 * img + h
                act.wait_ge(s["v_mm"], upto(n))
                if kind == "first":
                    act.wait_ge(s["const_made"], 14)
                src = bank("v", h).rearrange("p (b c) -> p b c", c=2 * HD)
                for odd in range(2):
                    mine = slice(HD * odd, HD * (odd + 1))
                    dst = vh[:, h, odd].rearrange("p a (b c) -> p (a b) c", c=2 * HD)
                    last = sc.activation(dst[:, :, mine], src[:, :, mine], ACT.Copy)
                last.then_inc(s["v_hi"], 1)

            def score(pair):
                def step(kind, img, h):
                    act.wait_ge(s["sub_made"], upto(2 * img + h, pair + 1, per=2))
                    sc.activation(e[:, h, :], e[:, h, :], ACT.Exp, scale=HD ** -0.5).then_inc(s["exp_made"], 1)
                return step

            def place_hi(pair):
                def step(kind, img, h):
                    n = 2 * img + h
                    act.wait_ge(s["et_made"], upto(n, pair + 1, per=2))
                    if due(value := upto(img - 1, 8, per=8, step=16)):
                        act.wait_ge(s[f"probs_in{h}{pair}"], value)
                    sc.activation(pt[:, h, pair, 0, :], et[:, h, :], ACT.Copy).then_inc(s["pt_hi"], 1)
                return step

            def pv1(kind, img, h):
                act.wait_ge(s["pv_win_mm"], upto(2 * img + h))
                sc.activation(oh[:, h, :], bank("pv0", h), ACT.Copy).then_inc(s["o_hi"], 1)

            def up(f):
                def step(kind, img, h):
                    n = 2 * img + h
                    act.wait_ge(s["up_mm"], upto(n, f + 1, per=FT))
                    if due(value := upto(n, f + 1 - 2, per=FT)):
                        act.wait_ge(s["hid_lo"], value)
                    sc.activation(hid[:, f % 2, :], bank(f"up{f}", h), ACT.Relu, bias=col(B1F + f)).then_inc(s["hid_made"], 1)
                return step

            def turn_q(kind, img, h):
                act.wait_ge(s["turn_q_mm"], upto(2 * img + h))
                sc.activation(qt[:, h, :], bank("turn_q", h)[:, 0:HALF // 2].bitcast(BF16), ACT.Copy).then_inc(s["qt_made"], 1)

            def ffn(kind, img, h):
                n = 2 * img + h
                act.wait_ge(s["ffn_mm"], upto(n))
                if due(value := upto(img - 1, step=16)):
                    act.wait_ge(s[f"stored{h}"], value)
                sc.activation(o_sb[:, h, :], bank("ffn", h), ACT.Identity, bias=col(BFB)).then_inc(s["o_made"], 1)
                act.wait_ge(s["o_made"], upto(n))
                act.dma_start(out[img, :, HALF * h:HALF * (h + 1)], o_sb[:, h, :]).then_inc(s[f"stored{h}"], 16)

            run(act, {"load_x": load_x, "gn2": gn2, "qg": global_hi("qg", qgh, QGB), "kg": global_hi("kg", kgh, KGB), "vg": vg, "st": st,
                      "turn_in": turned_hi("turn_in", "x_hi"), "q": q, "k": k, "v": v, "score0": score(0),
                      "score1": score(1), "place0": place_hi(0), "place1": place_hi(1), "pv1": pv1,
                      "turn_mid": turned_hi("turn_mid", "m_hi"), "up0": up(0), "up1": up(1), "up2": up(2),
                      "up3": up(3), "turn_q": turn_q, "ffn": ffn}, prologue)

        @block.vector
        def _(dve):
            v_ = nc.vector
            setup = [0]

            def link(ins):
                setup[0] += 1
                ins.then_inc(s["setup_dve"], 1)
                dve.wait_ge(s["setup_dve"], setup[0])

            def prologue():
                gn0(None, 0, 0)
                dve.wait_ge(s["weights_in"], 16 * 26)
                dve.wait_ge(s["const_made"], 10)
                link(v_.tensor_scalar(vb_full[:, 0, :], ones[:], col(VGB), None, ALU.mult))
                link(v_.tensor_scalar(vb_full[:, 1, :], ones[:], col(VB), None, ALU.mult))
                gn1(None, 0, 0)
                gn2(None, 0, 0)
                dve.wait_ge(s["setup_mm"], 1)
                for w in (QG, KG, Q, K, V, OUT):
                    link(v_.tensor_copy(wh[:, w, :], wraw[:, w, :]))
                    link(v_.tensor_tensor(wl[:, w, :], wraw[:, w, :], wh[:, w, :], ALU.subtract))
                link(v_.tensor_copy(wh[:, PVG, :], ps[:, 3, 0:P]))
                link(v_.tensor_tensor(wl[:, PVG, :], ps[:, 3, 0:P], wh[:, PVG, :], ALU.subtract))
                link(v_.tensor_tensor(rows[:, PROJR, :], ps[:, 4, 0:P], rows[:, PROJR, :], ALU.add))
                link(v_.tensor_tensor(rows[:, BO, :], ps[:, 4, P:2 * P], rows[:, BO, :], ALU.add))
                link(v_.tensor_tensor(cols[:, B1F:B1F + FT], ps[:, 5, 0:FT], cols[:, B1:B1 + FT], ALU.add))
                link(v_.tensor_tensor(rows[:, RB1, :], rows[:, RB1, :], rows[:, RB2, :], ALU.add))
                link(v_.tensor_scalar(w1raw, w1raw, col(LN1G), None, ALU.mult))
                for raw, hi, lo in ((w1raw, w1h, w1l), (w2raw, w2h, w2l)):
                    link(v_.tensor_copy(hi[:], raw))
                    link(v_.tensor_tensor(lo[:], raw, hi[:], ALU.subtract))
                link(v_.tensor_copy(ffnb16[:], col(FFNB)))
                link(v_.tensor_copy(col(BFB), ffnb16[:]))
                link(v_.reciprocal(col(R_IN), col(S_IN)))
                link(v_.reciprocal(col(R_K), col(S_K)))
                link(v_.tensor_tensor(col(S_BOTH), col(S_IN), col(S_K), ALU.mult))
                link(v_.tensor_scalar(kraw, kraw, col(R_K), None, ALU.mult))
                link(v_.tensor_scalar(kraw, kraw, E4M3_MAX, -E4M3_MAX, ALU.min, ALU.max))
                link(v_.tensor_scalar(expo[:, 0:P].bitcast(I32), kraw.bitcast(I32), EXP_MASK, None, ALU.bitwise_and))
                link(v_.tensor_scalar(expo[:, 0:P], expo[:, 0:P], E4M3_MIN_NORMAL, None, ALU.max))
                link(v_.scalar_tensor_tensor(kraw, expo[:, 0:P], ROUND_3_BITS, kraw, ALU.mult, ALU.add))
                link(v_.scalar_tensor_tensor(kraw, expo[:, 0:P], -ROUND_3_BITS, kraw, ALU.mult, ALU.add))
                link(v_.tensor_scalar(kraw, kraw, col(S_BOTH), None, ALU.mult))
                link(v_.tensor_copy(kh[:], kraw))
                link(v_.tensor_tensor(kl[:], kraw, kh[:], ALU.subtract))

            def gn0(kind, img, _):
                dve.wait_ge(s["x_in"], upto(img, step=16))
                v_.bn_stats(gst[:, 0, :], x_sb[:, 0:HALF])
                v_.bn_stats(gst[:, 1, :], x_sb[:, HALF:N]).then_inc(s["gn_stats"], 1)
                dve.wait_ge(s["gn_stats"], upto(img))
                v_.memset(spare[:], 0.0)
                v_.bn_aggr(gmv[:], gst[:].rearrange("p a b -> p (a b)")).then_inc(s["gn_mv"], 1)

            def gn1(kind, img, _):
                dve.wait_ge(s["gn_mm"], upto(img, 1, per=2))
                v_.tensor_copy(gt(GMEAN), bank("gn1", 0)[:, 0:1]).then_inc(s["gn_mean"], 1)
                dve.wait_ge(s["gn_mean"], upto(img))
                v_.tensor_tensor(gt(GDIFF), gmv[:, 0:1], gt(GMEAN), ALU.subtract).then_inc(s["gn_diff"], 1)
                dve.wait_ge(s["gn_diff"], upto(img))
                v_.scalar_tensor_tensor(gt(GVAR), gt(GDIFF), gt(GDIFF), gmv[:, 1:2], ALU.mult, ALU.add).then_inc(s["gn_var"], 1)

            def gn2(kind, img, _):
                dve.wait_ge(s["gn_mm"], upto(img, 2, per=2))
                v_.tensor_scalar(gt(GEPS), bank("gn2", 0)[:, 0:1], EPS, None, ALU.add).then_inc(s["gn_veps"], 1)
                dve.wait_ge(s["gn_pow"], upto(img))
                v_.tensor_tensor(gt(GSCALE), gt(GRSTD), col(GNW), ALU.mult).then_inc(s["gn_scale"], 1)
                dve.wait_ge(s["gn_scale"], upto(img))
                v_.scalar_tensor_tensor(gt(GNEG), gt(GSCALE), gt(GMEAN), col(GNB), ALU.mult, ALU.subtract).then_inc(s["gn_neg"], 1)
                dve.wait_ge(s["gn_neg"], upto(img))
                v_.tensor_scalar(gt(GBIAS), gt(GNEG), -1.0, None, ALU.mult).then_inc(s["gn_coef"], 1)
                dve.wait_ge(s["gn_coef"], upto(img))
                if due(value := upto(img - 1)):
                    dve.wait_ge(s["h_lo"], value)
                v_.tensor_scalar(h32[:], x_sb[:], gt(GSCALE), gt(GBIAS), ALU.mult, ALU.add).then_inc(s["h32_made"], 1)

            def global_lo(name, hi, lo, bias):
                def step(kind, img, c):
                    dve.wait_ge(s[name + "_hi"], upto(img, c + 1, per=2))
                    part = slice(HALF * c, HALF * (c + 1))
                    v_.scalar_tensor_tensor(lo[:, part], bank(name, c), col(bias), hi[:, part], ALU.add,
                                            ALU.subtract).then_inc(s[name + "_lo"], 1)
                return step

            def vg(kind, img, c):
                dve.wait_ge(s["vg_hi"], upto(img, c + 1, per=2))
                part = slice(HT * c, HT * (c + 1))
                v_.tensor_tensor(vgl[:, part, :], tiles(bank("vg", c)), vgh[:, part, 0:C], ALU.subtract).then_inc(s["vg_lo"], 1)

            def turn_x(kind, img, c):
                dve.wait_ge(s["turn_x_mm"], upto(img, c + 1, per=2))
                v_.tensor_tensor(xt[:, c], tiles(bank("turn_x", c)), row(PROJR), ALU.add).then_inc(s["xt_made"], 1)

            def row_max(kind, img, c):
                dve.wait_ge(s["max_mm"], upto(img, c + 1, per=2 * MT))
                v_.reduce_max(cm[:, c // 2, c % 2:c % 2 + 1], bank("max", c), X).then_inc(s["max_out"], 1)

            def make_shift(kind, img, c):
                dve.wait_ge(s["max_out"], upto(img, MT * (c + 1), per=2 * MT))
                v_.reduce_max(cmax[:], cm[:, HT * c:HT * (c + 1), :], X).then_inc(s["cmax_made"], 1)
                dve.wait_ge(s["cmax_made"], upto(img, c + 1, per=2))
                v_.tensor_copy(chi[:], cmax[:]).then_inc(s["chi_made"], 1)
                dve.wait_ge(s["chi_made"], upto(img, c + 1, per=2))
                if due(value := upto(img, c, per=2)):
                    dve.wait_ge(s["shift_turned"], value)
                v_.tensor_copy(cparts[:, 0:HT], chi[:])
                v_.tensor_tensor(cparts[:, HT:2 * HT], cmax[:], chi[:], ALU.subtract).then_inc(s["cparts_made"], 1)
                dve.wait_ge(s["shift_turned"], upto(img, c + 1, per=2))
                turned = ps[0:2 * HT, BANK["shift", c]:BANK["shift", c] + 1, 0:P].to_broadcast([2 * HT, HT, P])
                v_.tensor_tensor(shift[0:2 * HT, c], turned, sel[:], ALU.mult).then_inc(s["shift_made"], 1)

            def st(kind, img, c):
                dve.wait_ge(s["p_made"], upto(img, c + 1, per=2 * MT))
                if due(value := upto(img, c + 1 - PRING, per=2 * MT)):
                    dve.wait_ge(s["pv_mm"], value)
                v_.tensor_copy(ph[:, c % PRING, :], p32[:, c % PRING, :]).then_inc(s["p_hi"], 1)

            def pv(kind, img, c):
                if c % MT != MT - 1:
                    return
                h = c // MT
                dve.wait_ge(s["pv_mm"], upto(img, c + 1, per=2 * MT))
                acc = ps[:, PV_BANKS[0]:PV_BANKS[1] + 1, 0:2 * PVW].rearrange("p a (b c) -> p a b c", c=PVW)
                v_.reciprocal(rsum[:], acc[:, :, :, C]).then_inc(s["rsum_made"], 1)
                dve.wait_ge(s["rsum_made"], upto(img, h + 1, per=2))
                dve.wait_ge(s["xt_made"], upto(img, 2, per=2))
                if due(value := upto(2 * img + h - 2)):
                    dve.wait_ge(s["ffn_mm"], value)
                for j in range(HT):
                    last = v_.scalar_tensor_tensor(t[:, h, j, :], acc[:, j // 2, j % 2, 0:C], rsum[:, j // 2, j % 2:j % 2 + 1],
                                                   xt[:, h, j, :], ALU.mult, ALU.add)
                last.then_inc(s["t_made"], 1)

            def variance(src, n, k, h):
                for j in range(HT):
                    last = v_.bn_stats(stats[:, h, j, :], src[:, h, j, :])
                last.then_inc(s[f"ln_stats{k}"], 1)
                dve.wait_ge(s[f"ln_stats{k}"], upto(n))
                v_.memset(spare[:], 0.0)
                for j in range(HT):
                    last = v_.bn_aggr(mv[:, h, j, :], stats[:, h, j, :])
                last.then_inc(s[f"ln_mv{k}"], 1)
                dve.wait_ge(s[f"ln_mv{k}"], upto(n))
                v_.tensor_scalar(veps[:, h, :], mv[:, h, :, 1], EPS, None, ALU.add).then_inc(s[f"ln_veps{k}"], 1)

            def normalise(dst, src, n, k, h):
                dve.wait_ge(s[f"ln_pow{k}"], upto(n))
                for j in range(HT):
                    last = v_.tensor_scalar(dst[:, h, j, :], src[:, h, j, :], mv[:, h, j, 0:1], rstd[:, h, j:j + 1],
                                            ALU.subtract, ALU.mult)
                last.then_inc(s[f"norm_made{k}"], 1)

            def ln_in(kind, img, h):
                dve.wait_ge(s["t_made"], upto(2 * img + h))
                variance(t, 2 * img + h, 0, h)

            def norm_in(kind, img, h):
                normalise(y, t, 2 * img + h, 0, h)

            def turned_lo(name, hi_signal, signal):
                def step(kind, img, h):
                    dve.wait_ge(s[hi_signal], upto(2 * img + h))
                    v_.tensor_tensor(xl[:, h, :], bank(name, h), xh[:, h, :], ALU.subtract).then_inc(s[signal], 1)
                return step

            def q(kind, img, h):
                dve.wait_ge(s["q_hi"], upto(2 * img + h))
                v_.scalar_tensor_tensor(ql[:, h, :], bank("q", h), col(QB), qh[:, h, :], ALU.add,
                                        ALU.subtract).then_inc(s["q_lo"], 1)

            def k(kind, img, h):
                n = 2 * img + h
                dve.wait_ge(s["k_hi"], upto(n))
                if due(value := upto(img - 1, HEADS, per=HEADS, step=16)):
                    dve.wait_ge(s[f"keys_in{h}"], value)
                v_.scalar_tensor_tensor(kk[:, h, 1, :], bank("k", h), col(KB), kk[:, h, 0, :], ALU.add,
                                        ALU.subtract).then_inc(s["k_lo"], 1)

            def v(kind, img, h):
                dve.wait_ge(s["v_hi"], upto(2 * img + h))
                src = bank("v", h).rearrange("p (b c) -> p b c", c=2 * HD)
                for odd in range(2):
                    mine = slice(HD * odd, HD * (odd + 1))
                    hi = vh[:, h, odd].rearrange("p a (b c) -> p (a b) c", c=2 * HD)
                    lo = vl[:, h, odd].rearrange("p a (b c) -> p (a b) c", c=2 * HD)
                    last = v_.tensor_tensor(lo[:, :, mine], src[:, :, mine], hi[:, :, mine], ALU.subtract)
                last.then_inc(s["v_lo"], 1)

            def by_head(ap):
                return ap.rearrange("p (a b) -> p a b", b=WIN)

            def spread(ap):
                return ap.unsqueeze(2).to_broadcast([P, 2 * HEADS, WIN])

            def score(pair):
                def step(kind, img, h):
                    n = 2 * img + h
                    dve.wait_ge(s["score_mm"], upto(n, pair + 1, per=2))
                    v_.reduce_max(smax[:, h, :], by_head(bank(f"score{pair}", h)), X).then_inc(s["smax_made"], 1)
                    dve.wait_ge(s["smax_made"], upto(n, pair + 1, per=2))
                    v_.tensor_tensor(by_head(e[:, h, :]), by_head(bank(f"score{pair}", h)), spread(smax[:, h, :]),
                                     ALU.subtract).then_inc(s["sub_made"], 1)
                return step

            def prob(pair):
                def step(kind, img, h):
                    n = 2 * img + h
                    dve.wait_ge(s["exp_made"], upto(n, pair + 1, per=2))
                    v_.reduce_sum(ssum[:, h, :], by_head(e[:, h, :]), X).then_inc(s["ssum_made"], 1)
                    dve.wait_ge(s["ssum_made"], upto(n, pair + 1, per=2))
                    v_.reciprocal(srec[:, h, :], ssum[:, h, :]).then_inc(s["srec_made"], 1)
                    dve.wait_ge(s["srec_made"], upto(n, pair + 1, per=2))
                    v_.tensor_tensor(by_head(e[:, h, :]), by_head(e[:, h, :]), spread(srec[:, h, :]),
                                     ALU.mult).then_inc(s["prob_made"], 1)
                    dve.wait_ge(s["prob_made"], upto(n, pair + 1, per=2))
                    if pair:
                        dve.wait_ge(s["pt_lo"], upto(n, 1, per=2))
                    v_.transpose(et[:, h, :], e[:, h, :]).then_inc(s["et_made"], 1)
                return step

            def pv1(kind, img, h):
                dve.wait_ge(s["o_hi"], upto(2 * img + h))
                v_.tensor_tensor(ol[:, h, :], bank("pv0", h), oh[:, h, :], ALU.subtract).then_inc(s["o_lo"], 1)

            def out_proj(kind, img, h):
                n = 2 * img + h
                dve.wait_ge(s["out_mm"], upto(n))
                dve.wait_ge(s["xr_made"], upto(n))
                v_.tensor_tensor(y[:, h], tiles(bank("out", h)), res[:, h], ALU.add).then_inc(s["y1_made"], 1)
                dve.wait_ge(s["y1_made"], upto(n))
                variance(y, n, 1, h)

            def norm_mid(kind, img, h):
                normalise(y, y, 2 * img + h, 1, h)

            def up(f):
                def step(kind, img, h):
                    n = 2 * img + h
                    dve.wait_ge(s["hid_made"], upto(n, f + 1, per=FT))
                    if due(value := upto(n - 1)):
                        dve.wait_ge(s["down_mm"], value)
                    v_.tensor_copy(fh[:, f, :], hid[:, f % 2, :]).then_inc(s["hid_hi"], 1)
                return step

            def down(kind, img, h):
                n = 2 * img + h
                dve.wait_ge(s["down_mm"], upto(n))
                dve.wait_ge(s["r1_made"], upto(n))
                v_.tensor_tensor(y[:, h], tiles(bank("down", h)), res[:, h], ALU.add).then_inc(s["y2_made"], 1)
                dve.wait_ge(s["y2_made"], upto(n))
                variance(y, n, 2, h)

            def norm_out(kind, img, h):
                normalise(y, y, 2 * img + h, 2, h)

            def ln_q(kind, img, h):
                dve.wait_ge(s["t2_made"], upto(2 * img + h))
                variance(t, 2 * img + h, 3, h)

            def quant(kind, img, h):
                n = 2 * img + h
                dve.wait_ge(s["ln_pow3"], upto(n))
                v_.tensor_scalar(rstd[:, h, :], rstd[:, h, :], col(R_IN), None, ALU.mult).then_inc(s["scaled"], 1)
                dve.wait_ge(s["scaled"], upto(n))
                for j in range(HT):
                    last = v_.tensor_scalar(z[:, P * j:P * (j + 1)], t[:, h, j, :], mv[:, h, j, 0:1], rstd[:, h, j:j + 1],
                                            ALU.subtract, ALU.mult)
                last.then_inc(s["z_made"], 1)
                dve.wait_ge(s["z_made"], upto(n))
                v_.tensor_scalar(z[:], z[:], E4M3_MAX, -E4M3_MAX, ALU.min, ALU.max).then_inc(s["clipped"], 1)
                dve.wait_ge(s["clipped"], upto(n))
                v_.tensor_scalar(expo[:].bitcast(I32), z[:].bitcast(I32), EXP_MASK, None, ALU.bitwise_and).then_inc(s["expo_made"], 1)
                dve.wait_ge(s["expo_made"], upto(n))
                v_.tensor_scalar(expo[:], expo[:], E4M3_MIN_NORMAL, None, ALU.max).then_inc(s["expo_low"], 1)
                dve.wait_ge(s["expo_low"], upto(n))
                v_.scalar_tensor_tensor(z[:], expo[:], ROUND_3_BITS, z[:], ALU.mult, ALU.add).then_inc(s["rounded"], 1)
                dve.wait_ge(s["rounded"], upto(n))
                v_.scalar_tensor_tensor(qz[:, h].rearrange("p a b -> p (a b)"), expo[:], -ROUND_3_BITS, z[:], ALU.mult,
                                        ALU.add).then_inc(s["qz_made"], 1)

            run(dve, {"gn0": gn0, "gn1": gn1, "gn2": gn2, "qg": global_lo("qg", qgh, qgl, QGB),
                      "kg": global_lo("kg", kgh, kgl, KGB), "vg": vg, "turn_x": turn_x, "max": row_max,
                      "shift": make_shift, "st": st, "pv": pv, "ln_in": ln_in, "norm_in": norm_in,
                      "turn_in": turned_lo("turn_in", "x_hi", "x_lo"), "q": q, "k": k, "v": v, "score0": score(0),
                      "score1": score(1), "prob0": prob(0), "prob1": prob(1), "pv1": pv1, "out": out_proj,
                      "norm_mid": norm_mid, "turn_mid": turned_lo("turn_mid", "m_hi", "m_lo"), "up0": up(0), "up1": up(1),
                      "up2": up(2), "up3": up(3), "down": down, "norm_out": norm_out, "ln_q": ln_q,
                      "quant": quant}, prologue)

        @block.tensor
        def _(pe):
            mm = nc.tensor.matmul

            def claim(kind, img, name, index):
                if (kind, name, index) not in before:
                    return
                pname, pindex, back = before[kind, name, index]
                signal, per, by_half = RELEASE[pname]
                if by_half:
                    k = int(pname[-1]) + 1 if per > 1 else 1
                    pe.wait_ge(s[signal], upto(2 * (img - back) + pindex, k, per=per))
                else:
                    pe.wait_ge(s[signal], upto(img - back, pindex + 1, per=per))

            def three(dst, lhi, llo, rhi, rlo, first=True, last=True, **kw):
                mm(dst, lhi, rhi, start=first, stop=False, **kw)
                mm(dst, lhi, rlo, start=False, stop=False, **kw)
                return mm(dst, llo, rhi, start=False, stop=last, **kw)

            def prologue():
                gn1(None, 0, 0)
                pe.wait_ge(s["weights_in"], 16 * 26)
                pe.wait_ge(s["setup_dve"], 2)
                mm(ps[:, 3, 0:P], wraw[:, VG, :], wraw[:, PROJ, :], start=True, stop=True)
                mm(ps[:, 4, 0:P], vb_full[:, 0, :], wraw[:, PROJ, :], start=True, stop=True)
                mm(ps[:, 4, P:2 * P], vb_full[:, 1, :], wraw[:, OUT, :], start=True, stop=True)
                for f in range(FT):
                    last = mm(ps[:, 5, f:f + 1], w1raw[:, P * f:P * (f + 1)], col(LN1B), start=True, stop=True)
                last.then_inc(s["setup_mm"], 1)
                gn2(None, 0, 0)
                pe.wait_ge(s["setup_dve"], SETUP_STEPS)

            def gn1(kind, img, _):
                claim(kind or "prologue", img, "gn1", 0)
                if kind is None:
                    pe.wait_ge(s["const_mask"], 6)
                pe.wait_ge(s["gn_mv"], upto(img))
                mm(bank("gn1", 0)[:, 0:1], group_mean[:], gmv[:, 0:1], start=True, stop=True).then_inc(s["gn_mm"], 1)

            def gn2(kind, img, _):
                claim(kind or "prologue", img, "gn2", 0)
                pe.wait_ge(s["gn_var"], upto(img))
                mm(bank("gn2", 0)[:, 0:1], group_mean[:], gt(GVAR), start=True, stop=True).then_inc(s["gn_mm"], 1)

            def project(name, w):
                def step(kind, img, c):
                    claim(kind, img, name, c)
                    pe.wait_ge(s["h_hi"], upto(img))
                    pe.wait_ge(s["h_lo"], upto(img))
                    part = slice(HALF * c, HALF * (c + 1))
                    three(bank(name, c), wh[:, w, :], wl[:, w, :], hh[:, part], hl[:, part]).then_inc(s[name + "_mm"], 1)
                return step

            def vg(kind, img, c):
                claim(kind, img, "vg", c)
                for j in range(HT):
                    part = slice(HALF * c + P * j, HALF * c + P * (j + 1))
                    last = three(bank("vg", c)[:, P * j:P * (j + 1)], hh[:, part], hl[:, part], wh[:, PVG, :], wl[:, PVG, :])
                last.then_inc(s["vg_mm"], 1)

            def turn_x(kind, img, c):
                claim(kind, img, "turn_x", c)
                for j in range(HT):
                    part = slice(HALF * c + P * j, HALF * c + P * (j + 1))
                    last = nc.tensor.transpose(bank("turn_x", c)[:, P * j:P * (j + 1)], x_sb[:, part], identf[:])
                last.then_inc(s["turn_x_mm"], 1)

            def row_max(kind, img, c):
                claim(kind, img, "max", c)
                pe.wait_ge(s["qg_hi"], upto(img, c // MT + 1, per=2))
                pe.wait_ge(s["kg_hi"], upto(img, c % 2 + 1, per=2))
                mm(bank("max", c), qgh[:, P * (c // 2):P * (c // 2 + 1)], kgh[:, HALF * (c % 2):HALF * (c % 2 + 1)],
                   start=True, stop=True).then_inc(s["max_mm"], 1)

            def turn_shift(kind, img, c):
                claim(kind, img, "shift", c)
                pe.wait_ge(s["cparts_made"], upto(img, c + 1, per=2))
                nc.tensor.transpose(bank("shift", c)[:, 0:P], cparts[:], identf[:]).then_inc(s["shift_turned"], 1)

            def st(kind, img, c):
                h, j = divmod(c, MT)
                claim(kind, img, "st", c)
                pe.wait_ge(s["shift_made"], upto(img, h + 1, per=2))
                pe.wait_ge(s["qg_lo"], upto(img, h + 1, per=2))
                pe.wait_ge(s["kg_lo"], upto(img, j // HT + 1, per=2))
                keys, queries = slice(P * j, P * (j + 1)), slice(HALF * h, HALF * (h + 1))
                mm(bank("st", c), minus1[:], shift[:, h].rearrange("p a b -> p (a b)"), start=True, stop=False)
                three(bank("st", c), kgh[:, keys], kgl[:, keys], qgh[:, queries], qgl[:, queries],
                      first=False).then_inc(s["st_mm"], 1)

            def pv(kind, img, c):
                h, j = divmod(c, MT)
                if j == 0:
                    if due(value := upto(2 * img + h - 1)):
                        pe.wait_ge(s["t_made"], value)
                    pe.wait_ge(s["vg_lo"], upto(img, 2, per=2))
                pe.wait_ge(s["p_hi"], upto(img, c + 1, per=2 * MT))
                pe.wait_ge(s["p_lo"], upto(img, c + 1, per=2 * MT))
                for q in range(HT):
                    b, at = PV_BANKS[q // 2], PVW * (q % 2)
                    part = slice(P * q, P * (q + 1))
                    mm(ps[:, b, at:at + PVW], ph[:, c % PRING, part], vgh[:, j, :], start=j == 0 and q % 2 == 0,
                       stop=False, skip_group_check=True)
                    mm(ps[:, b, at:at + C], ph[:, c % PRING, part], vgl[:, j, :], start=False, stop=False,
                       skip_group_check=True)
                    last = mm(ps[:, b, at:at + PVW], pl[:, c % PRING, part], vgh[:, j, :], start=False,
                              stop=j == MT - 1, skip_group_check=True)
                last.then_inc(s["pv_mm"], 1)

            def turn(name, src, k):
                def step(kind, img, h):
                    n = 2 * img + h
                    claim(kind, img, name, h)
                    pe.wait_ge(s[f"norm_made{k}"], upto(n))
                    for j in range(HT):
                        last = nc.tensor.transpose(bank(name, h)[:, P * j:P * (j + 1)], src[:, h, j, :], identf[:])
                    last.then_inc(s[name + "_mm"], 1)
                return step

            def q(kind, img, h):
                n = 2 * img + h
                claim(kind, img, "q", h)
                pe.wait_ge(s["x_lo"], upto(n))
                three(bank("q", h), wh[:, Q, :], wl[:, Q, :], xh[:, h, :], xl[:, h, :]).then_inc(s["q_mm"], 1)

            def k(kind, img, h):
                claim(kind, img, "k", h)
                three(bank("k", h), wh[:, K, :], wl[:, K, :], xh[:, h, :], xl[:, h, :]).then_inc(s["k_mm"], 1)

            def v(kind, img, h):
                claim(kind, img, "v", h)
                for j in range(HT):
                    part = slice(P * j, P * (j + 1))
                    last = three(bank("v", h)[:, part], xh[:, h, part], xl[:, h, part], wh[:, V, :], wl[:, V, :])
                last.then_inc(s["v_mm"], 1)

            def score(pair):
                def step(kind, img, h):
                    n = 2 * img + h
                    name = f"score{pair}"
                    claim(kind, img, name, h)
                    pe.wait_ge(s["q_lo"], upto(n))
                    pe.wait_ge(s[f"keys_in{h}"], upto(img, HEADS, per=HEADS, step=16))
                    for tt in range(2):
                        for m, (left, part) in enumerate(((qh, 0), (qh, 1), (ql, 0))):
                            for w in range(4):
                                tok = P * (2 * pair + tt) + WIN * w
                                last = mm(ps[WIN * w:WIN * (w + 1), BANK[name, h], HALF // 2 * tt:HALF // 2 * (tt + 1)],
                                          left[:, h, tok:tok + WIN], kbd[:, h, :, part, tok:tok + WIN],
                                          start=m == 0, stop=m == 2)
                    last.then_inc(s["score_mm"], 1)
                return step

            def pv_win(pair):
                def step(kind, img, h):
                    n = 2 * img + h
                    if pair == 0:
                        claim(kind, img, "pv0", h)
                        pe.wait_ge(s["v_lo"], upto(n))
                    pe.wait_ge(s[f"probs_in{h}{pair}"], upto(img, 8, per=8, step=16))
                    for j in (2 * pair, 2 * pair + 1):
                        for m, (val, part, odd) in enumerate(((vh, 0, 0), (vl, 0, 0), (vh, 1, 0), (vh, 0, 1), (vl, 0, 1), (vh, 1, 1))):
                            for two in range(4):
                                head = 2 * two + odd
                                last = mm(ps[WIN * two:WIN * (two + 1), BANK["pv0", h], P * j:P * (j + 1)],
                                          val[:, h, odd, j, WIN * two:WIN * (two + 1)],
                                          ptbd[:, h, part, j, :, WIN * head:WIN * (head + 1)],
                                          start=m == 0, stop=m == 5)
                    if pair == 1:
                        last.then_inc(s["pv_win_mm"], 1)
                return step

            def out_proj(kind, img, h):
                claim(kind, img, "out", h)
                pe.wait_ge(s["o_lo"], upto(2 * img + h))
                for j in range(HT):
                    part = slice(P * j, P * (j + 1))
                    last = three(bank("out", h)[:, part], oh[:, h, part], ol[:, h, part], wh[:, OUT, :], wl[:, OUT, :])
                last.then_inc(s["out_mm"], 1)

            def up(f):
                def step(kind, img, h):
                    claim(kind, img, f"up{f}", h)
                    pe.wait_ge(s["m_lo"], upto(2 * img + h))
                    part = slice(P * f, P * (f + 1))
                    three(bank(f"up{f}", h), w1h[:, part], w1l[:, part], xh[:, h, :], xl[:, h, :]).then_inc(s["up_mm"], 1)
                return step

            def down(kind, img, h):
                n = 2 * img + h
                claim(kind, img, "down", h)
                pe.wait_ge(s["hid_lo"], upto(n, FT, per=FT))
                for j in range(HT):
                    part = slice(P * j, P * (j + 1))
                    for f in range(FT):
                        last = three(bank("down", h)[:, part], fh[:, f, part], fl[:, f, part], w2h[:, f, :], w2l[:, f, :],
                                     first=f == 0, last=f == FT - 1)
                last.then_inc(s["down_mm"], 1)

            def turn_q(kind, img, h):
                claim(kind, img, "turn_q", h)
                pe.wait_ge(s["qz_made"], upto(2 * img + h))
                dst = bank("turn_q", h)[:, 0:HALF // 2].bitcast(BF16)
                for j in range(HT):
                    last = nc.tensor.transpose(dst[:, P * j:P * (j + 1)], qz[:, h, j, :], identh[:])
                last.then_inc(s["turn_q_mm"], 1)

            def ffn(kind, img, h):
                n = 2 * img + h
                claim(kind, img, "ffn", h)
                pe.wait_ge(s["qt_made"], upto(n))
                for j in range(HT):
                    part = slice(P * j, P * (j + 1))
                    dst = bank("ffn", h)[:, part]
                    mm(dst, t[:, h, j, :], identf[:], is_transpose=True, start=True, stop=False)
                    mm(dst, kh[:], qt[:, h, part], start=False, stop=False)
                    last = mm(dst, kl[:], qt[:, h, part], start=False, stop=True)
                last.then_inc(s["ffn_mm"], 1)

            run(pe, {"gn1": gn1, "gn2": gn2, "qg": project("qg", QG), "kg": project("kg", KG), "vg": vg, "turn_x": turn_x,
                     "max": row_max, "shift": turn_shift, "st": st, "pv": pv, "turn_in": turn("turn_in", y, 0), "q": q,
                     "k": k, "v": v, "score0": score(0), "score1": score(1), "pv0": pv_win(0), "pv1": pv_win(1),
                     "out": out_proj, "turn_mid": turn("turn_mid", y, 1), "up0": up(0), "up1": up(1), "up2": up(2),
                     "up3": up(3), "down": down, "turn_q": turn_q, "ffn": ffn}, prologue)


SETUP_STEPS = 2 + 12 + 7 + 4 + 2 + 3 + 1 + 5 + 1 + 2


def kernel(**inputs):
    import concourse.bacc as _bacc
    from concourse.bass_utils import run_bass_kernel_spmd as _run

    def arr(name):
        return np.ascontiguousarray(inputs[name])

    qkv_w = arr("L0_conv_qkv_w")
    arrays = {
        "x": arr("x").reshape(IMAGES, C, N),
        "qkv_w_t": np.ascontiguousarray(qkv_w.T), "v_w": np.ascontiguousarray(qkv_w[2 * C:]),
        "proj_w_t": np.ascontiguousarray(arr("L0_conv_proj_w").T),
        "in_w_t": np.ascontiguousarray(arr("L1_attn_in_proj_w").T),
        "out_w_t": np.ascontiguousarray(arr("L1_attn_out_w").T),
        "w1_t": np.ascontiguousarray(arr("L1_attn_w1").T), "w2_t": np.ascontiguousarray(arr("L1_attn_w2").T),
        "kernel": arr("L1_ffn_kernel"), "qkv_b": arr("L0_conv_qkv_b"), "proj_b": arr("L0_conv_proj_b"),
        "gn_w": arr("L0_conv_gn_w"), "gn_b": arr("L0_conv_gn_b"), "in_b": arr("L1_attn_in_proj_b"),
        "out_b": arr("L1_attn_out_b"), "ln1_g": arr("L1_attn_ln1_g"), "ln1_b": arr("L1_attn_ln1_b"),
        "b1": arr("L1_attn_b1"), "b2": arr("L1_attn_b2"), "ln2_g": arr("L1_attn_ln2_g"), "ln2_b": arr("L1_attn_ln2_b"),
        "ffn_b": arr("L1_ffn_bias"), "s_in": arr("L1_ffn_input_scale"), "s_k": arr("L1_ffn_kernel_scale"),
    }
    nc = _bacc.Bacc("TRN2", target_bir_lowering=False, num_devices=1)
    aps = {n: nc.dram_tensor("in_" + n, v.shape, F32, kind="ExternalInput").ap() for n, v in arrays.items()}
    out = nc.dram_tensor("out_y", (IMAGES, C, N), F32, kind="ExternalOutput").ap()
    build(nc, aps, out)
    r = _run(nc, [{"in_" + n: v for n, v in arrays.items()}], core_ids=[0])
    return r.results[0]["out_y"].reshape(IMAGES, C, 32, 32)
```

```python
from contextlib import ExitStack

import concourse.bass as bass
import numpy as np
from concourse import mybir

F32 = mybir.dt.float32
F16 = mybir.dt.float16
BF16 = mybir.dt.bfloat16
I32 = mybir.dt.int32
ALU = mybir.AluOpType
ACT = mybir.ActivationFunctionType
X = mybir.AxisListType.X

IMAGES, C, N = 32, 128, 1024
P = 128
HALF = 512
HT = HALF // P
MT = N // P
GROUP = C // 32
HEADS, HD, WIN = 8, 16, 32
FF = 4 * C
FT = FF // P
PVW = C + 1
PRING = 4
EPS = 1e-5
E4M3_MAX = 448.0
EXP_MASK = 0x7F800000
E4M3_MIN_NORMAL = 2.0 ** -6
ROUND_3_BITS = 1.5 * 2.0 ** 20

PROGRAM = {
    "pe": """
        pv:11- kg:0 pv:12- pv:13- pv:14- pv:15- kg:1 qg:0 vg:0 pv0:0- max:0 max:1 max:2 max:3 turn_in:1-
        pv1:0- max:4 max:5 k:1- max:6 out:0- max:7 q:1- v:1- qg:1 shift:0 vg:1 max:8 st:0 turn_mid:0-
        score0:1- st:1 up0:0- max:9 up1:0- max:10 max:11 up2:0- score1:1- up3:0- st:2 st:3 pv:0 down:0- st:4
        max:12 st:5 pv0:1- pv1:1- max:13 pv:1 pv:2 out:1- st:6 st:7 max:14 pv:3 max:15 turn_x:0 turn_mid:1-
        turn_x:1 pv:4 pv:5 up0:1- up1:1- shift:1 pv:6 up2:1- pv:7 turn_q:0- up3:1- st:8 ffn:0- st:9 down:1-
        st:10 st:11 turn_in:0 k:0 q:0 st:12 v:0 gn1:0 pv:8 pv:9 gn2:0 st:13 st:14 st:15 score0:0 score1:0
        turn_q:1- pv:10 ffn:1-""",
    "act": """
        kg:0 score1:0- place1:0- kg:1 qg:0 vg:0 norm_in:1- turn_in:1- pv1:0- k:1- qg:1 q:1- v:1- norm_mid:0-
        vg:1 turn_mid:0- st:0 st:1 score0:1- up0:0- up1:0- up2:0- place0:1- score1:1- up3:0- place1:1- st:2
        st:3 st:4 st:5 pv1:1- norm_out:0- st:6 st:7 norm_mid:1- turn_mid:1- quant:0- up0:1- up1:1- up2:1-
        turn_q:0- up3:1- st:8 load_x:0 st:9 ffn:0- norm_in:0 st:10 turn_in:0 norm_out:1- st:11 k:0 q:0 v:0
        st:12 quant:1- gn2:0 st:13 turn_q:1- score0:0 st:14 st:15 ffn:1- place0:0""",
    "dve": """
        st:13- prob0:0- score1:0- st:15- kg:0 prob1:0- pv:15- ln_in:1- kg:1 qg:0 vg:0 max:0 max:1 max:2
        max:3 turn_in:1- max:4 max:5 pv1:0- k:1- max:6 out:0- max:7 maxima:0 qg:1 shift:0 q:1- max:8 v:1-
        vg:1 turn_mid:0- score0:1- max:9 prob0:1- score1:1- max:10 prob1:1- max:11 st:1 down:0- st:3 pv1:1-
        max:12 st:5 out:1- max:13 ln_q:0- max:14 max:15 st:7 turn_x:0 turn_mid:1- maxima:1 quant:0- shift:1
        turn_x:1 pv:7 ln_in:0 down:1- turn_in:0 st:9 gn0:0 st:11 k:0 q:0 ln_q:1- gn1:0 v:0 gn2:0 quant:1-
        score0:0""",
    "pool": """
        place0:0- st:15- place1:0- ln_in:1- out:0- norm_mid:0- st:0 up0:0- up1:0- up2:0- place0:1- up3:0-
        place1:1- st:1 st:2 st:3 down:0- st:4 norm_out:0- out:1- st:5 ln_q:0- norm_mid:1- st:6 st:7 up0:1-
        up1:1- up2:1- up3:1- ln_in:0 st:8 down:1- norm_out:1- st:9 ln_q:1- gn2:0 st:10 st:11 st:12 st:13
        st:14""",
    "sp": """
        place1:0- k:1- place0:1- place1:1- k:0 place0:0""",
}


def order(engine):
    for word in PROGRAM[engine].split():
        name, index = word.rstrip("-").split(":")
        yield name, int(index), int(word.endswith("-"))


ORDER = {engine: list(order(engine)) for engine in PROGRAM}
NEXT = ("load_x", "gn0", "gn1", "gn2")

GLOBAL_BANKS, LAYER_BANKS, PV_BANKS = (0, 1, 2), (3, 4, 5), (6, 7)
GLOBAL_USES = ("qg", "kg", "vg", "turn_x", "max", "shift", "st", "gn1", "gn2")
LAYER_USES = ("turn_in", "q", "k", "v", "score0", "score1", "pv0", "out", "turn_mid", "up0", "up1",
              "up2", "up3", "down", "turn_q", "ffn")

RELEASE = {
    "qg": ("qg_lo", 2, False), "kg": ("kg_lo", 2, False), "vg": ("vg_lo", 2, False),
    "turn_x": ("xt_made", 2, False), "max": ("max_out", 2 * MT, False), "shift": ("shift_made", 2, False),
    "st": ("p_made", 2 * MT, False), "gn1": ("gn_mean", 1, False), "gn2": ("gn_veps", 1, False),
    "turn_in": ("x_lo", 1, True), "q": ("q_lo", 1, True), "k": ("k_lo", 1, True), "v": ("v_lo", 1, True),
    "score0": ("sub_made", 2, True), "score1": ("sub_made", 2, True), "pv0": ("o_lo", 1, True),
    "out": ("y1_made", 1, True), "turn_mid": ("m_lo", 1, True), "up0": ("hid_made", FT, True),
    "up1": ("hid_made", FT, True), "up2": ("hid_made", FT, True), "up3": ("hid_made", FT, True),
    "down": ("y2_made", 1, True), "turn_q": ("qt_made", 1, True), "ffn": ("o_made", 1, True),
}


def bank_table():
    bank, turn = {}, {GLOBAL_USES: 0, LAYER_USES: 0}
    for name, index, _ in ORDER["pe"]:
        for uses, banks in ((GLOBAL_USES, GLOBAL_BANKS), (LAYER_USES, LAYER_BANKS)):
            if name in uses:
                bank[name, index] = banks[turn[uses] % 3]
                turn[uses] += 1
    return bank


BANK = bank_table()


def steps_of(engine, new, old, nxt):
    for name, index, lag in ORDER[engine]:
        if (name in NEXT and nxt) or (name not in NEXT and (old if lag else new)):
            yield name, index, -lag if name not in NEXT else 1


def tenants(images):
    holder, table = {}, {}

    def iteration(kind, i, steps):
        for name, index, off in steps:
            if (name, index) in BANK:
                b, img = BANK[name, index], i + off
                if b in holder:
                    pname, pindex, pimg = holder[b]
                    table[kind, name, index] = (pname, pindex, img - pimg)
                holder[b] = (name, index, img)

    iteration("prologue", -1, [("gn1", 0, 1), ("gn2", 0, 1)])
    iteration("first", 0, steps_of("pe", True, False, True))
    iteration("second", 1, steps_of("pe", True, True, True))
    for i in range(2, images - 1):
        iteration("steady", i, steps_of("pe", True, True, True))
    iteration("last", images - 1, steps_of("pe", True, True, False))
    iteration("tail", images, steps_of("pe", False, True, False))
    return table


def build(nc, a, out, images=IMAGES):
    ctx = ExitStack()
    with ctx:
        def sb(name, shape, dt=F32):
            return ctx.enter_context(nc.sbuf_tensor(name, shape, dt))

        def sem(name):
            return ctx.enter_context(nc.semaphore(name))

        QG, KG, VG, PROJ, Q, K, V, OUT, PVG = range(9)
        wh, wl = sb("wh", [P, 9, P], F16), sb("wl", [P, 9, P], BF16)
        w1h, w1l = sb("w1h", [P, FF], F16), sb("w1l", [P, FF], BF16)
        w2h, w2l = sb("w2h", [P, FT, P], F16), sb("w2l", [P, FT, P], BF16)
        kh, kl = sb("kh", [P, P], F16), sb("kl", [P, P], BF16)
        cols = sb("cols", [P, 26])
        (QGB, KGB, VGB, PROJB, GNW, GNB, QB, KB, VB, LN1B, FFNB, B1) = range(12)
        B1F, BFB, LN1G, S_IN, S_K, R_IN, R_K, S_BOTH = 15, 19, 20, 21, 22, 23, 24, 25

        def col(c):
            return cols[:, c:c + 1]

        spare = sb("spare", [P, 1])
        ffnb16 = sb("ffnb16", [P, 1], BF16)
        BO, RG1, RB1, RB2, RG2, RBL2, PROJR = range(7)
        rows = sb("rows", [P, 7, P])

        def row(r):
            return rows[:, r:r + 1, :].to_broadcast([P, HT, P])

        identf, identh = sb("identf", [P, P]), sb("identh", [P, P], BF16)
        group_mean = sb("group_mean", [P, P])
        sel = sb("sel", [2 * HT, HT, P])
        minus1 = sb("minus1", [P, P], BF16)
        halfpow = sb("halfpow", [P, HT])
        ones16 = sb("ones16", [P, P], BF16)
        BIAS_OUT, BIAS_DOWN = range(2)
        bias16 = sb("bias16", [P, 2, P], BF16)

        x_sb = sb("x_sb", [P, N])
        xt = sb("xt", [P, 2, HT, P])
        gst, gmv = sb("gst", [P, 2, 6]), sb("gmv", [P, 2])
        GMEAN, GDIFF, GVAR, GEPS, GRSTD, GSCALE, GNEG, GBIAS = range(8)
        gtmp = sb("gtmp", [P, 8])

        def gt(c):
            return gtmp[:, c:c + 1]

        h32 = sb("h32", [P, N])
        hh, hl = sb("hh", [P, N], F16), sb("hl", [P, N], F16)
        qgh, qgl = sb("qgh", [P, N], F16), sb("qgl", [P, N], F16)
        kgh, kgl = sb("kgh", [P, N], F16), sb("kgl", [P, N], F16)
        vgh, vgl = sb("vgh", [P, MT, PVW], F16), sb("vgl", [P, MT, P], F16)
        cm = sb("cm", [P, MT, 2])
        cmax = sb("cmax", [P, HT])
        chi = sb("chi", [P, HT], BF16)
        cparts = sb("cparts", [P, P])
        shift = sb("shift", [P, 2, HT, P], BF16)
        p32 = sb("p32", [P, PRING, HALF])
        ph, pl = sb("ph", [P, PRING, HALF], F16), sb("pl", [P, PRING, HALF], F16)
        rsum = sb("rsum", [P, 2, 2])

        t = sb("t", [P, 2, HT, P])
        stats, mv = sb("stats", [P, 2, HT, 6]), sb("mv", [P, 2, HT, 2])
        veps, rstd = sb("veps", [P, 2, HT]), sb("rstd", [P, 2, HT])
        nmean, nshift = sb("nmean", [P, 2, HT]), sb("nshift", [P, 2, HT])
        xh, xl = sb("xh", [P, 2, HALF], F16), sb("xl", [P, 2, HALF], F16)
        qh, ql = sb("qh", [P, 2, HALF], F16), sb("ql", [P, 2, HALF], F16)
        kk = sb("kk", [P, 2, 2, HALF], F16)
        kbd = sb("kbd", [P, 2, HEADS, 2, HALF], F16)
        vh, vl = sb("vh", [P, 2, 2, HT, P], F16), sb("vl", [P, 2, 2, HT, P], F16)
        smax, ssum, srec = sb("smax", [P, 2, 16]), sb("ssum", [P, 2, 16]), sb("srec", [P, 2, 16])
        e, et = sb("e", [P, 2, HALF]), sb("et", [P, 2, HALF])
        pt = sb("pt", [P, 2, 2, 2, 2, HALF // 2], F16)
        ptbd = sb("ptbd", [P, 2, HT, 4, 2, HALF // 2], F16)
        oh, ol = sb("oh", [P, 2, HALF], F16), sb("ol", [P, 2, HALF], F16)
        y = sb("y", [P, 2, HT, P])
        res = sb("res", [P, 2, HT, P])
        hid = sb("hid", [P, 2, HALF])
        fh, fl = sb("fh", [P, FT, HALF], F16), sb("fl", [P, FT, HALF], F16)
        z, expo = sb("z", [P, 2, HALF]), sb("expo", [P, HALF])
        qz = sb("qz", [P, 2, HT, P], BF16)
        qt = sb("qt", [P, 2, HALF], BF16)
        o_sb = sb("o_sb", [P, 2, HALF])
        wraw = xt[:].rearrange("p a b c -> p (a b) c")
        w1raw, w2raw, kraw = e[:, 0, :], e[:, 1, :].rearrange("p (a b) -> p a b", b=P), et[:, 0, 0:P]
        ones = p32[:, 0, 0:P]
        vb_full = p32[:, 1, 0:2 * P].rearrange("p (a b) -> p a b", b=P)
        part16 = pl[:, 0, 0:P].bitcast(BF16)
        ps = ctx.enter_context(nc.psum_tensor("ps", [P, 8, HALF], F32))

        def bank(name, index):
            return ps[:, BANK[name, index], :]

        def tiles(ap):
            return ap.rearrange("p (a b) -> p a b", b=P)

        s = {n: sem(n) for n in """weights_in const_made const_mask setup_dve setup_mm
            x_in gn_stats gn_mv gn_mm gn_mean gn_diff gn_var gn_veps gn_pow gn_scale gn_neg gn_coef h32_made h_hi h_lo
            qg_mm kg_mm vg_mm turn_x_mm qg_hi kg_hi vg_hi qg_lo kg_lo vg_lo xt_made
            max_mm max_out cmax_made chi_made cparts_made shift_turned shift_made
            st_mm p_made p_hi0 p_hi1 p_lo pv_mm rsum_made t_made
            turn_in_mm turn_mid_mm x_hi x_lo q_mm k_mm v_mm
            q_hi q_lo k_hi k_lo v_hi v_lo score_mm smax_made sub_made exp_made ssum_made srec_made prob_made
            et_made pt_hi pt_lo pv_win_mm o_hi o_lo out_mm y1_made r1_made m_hi m_lo
            up_mm hid_made hid_hi hid_lo down_mm y2_made t2a_made t2b_made t2_made scaled clipped
            expo_made expo_low rounded qz_made turn_q_mm qt_made ffn_mm o_made""".split()}
        s.update({n: sem(n) for h in range(2) for n in (f"keys_in{h}", f"probs_in{h}0", f"probs_in{h}1", f"stored{h}")})
        s.update({f"{n}{k}": sem(f"{n}{k}") for k in range(4) for n in ("ln_stats", "ln_mv", "ln_veps", "ln_pow", "ln_shift", "norm_made")})

        def upto(unit, k=1, per=1, step=1):
            return (unit * per + k) * step

        def due(value):
            return not isinstance(value, int) or value > 0

        before = tenants(images)
        block = ctx.enter_context(nc.Block())

        def run(engine, key, table, prologue):
            prologue()

            def iteration(kind, i, new, old, nxt):
                for name, index, off in steps_of(key, new, old, nxt):
                    if name in table:
                        table[name](kind, i + off, index)

            iteration("first", 0, True, False, True)
            iteration("second", 1, True, True, True)
            with engine.Fori(2, images - 1) as i:
                iteration("steady", i, True, True, True)
            iteration("last", images - 1, True, True, False)
            iteration("tail", images, False, True, False)

        @block.sync
        def _(sp):
            def load(dst, src):
                sp.dma_start(dst, src).then_inc(s["weights_in"], 16)

            def prologue():
                sp.dma_start(x_sb[:, :], a["x"][0]).then_inc(s["x_in"], 16)
                load(wraw[:, QG:QG + 2, :].rearrange("p a b -> p (a b)"), a["qkv_w_t"][:, 0:2 * P])
                load(wraw[:, VG, :], a["v_w"])
                load(wraw[:, PROJ, :], a["proj_w_t"])
                load(wraw[:, Q:Q + 3, :].rearrange("p a b -> p (a b)"), a["in_w_t"])
                load(wraw[:, OUT, :], a["out_w_t"])
                load(w1raw, a["w1_t"])
                load(w2raw, a["w2_t"].rearrange("(t p) d -> p t d", p=P))
                load(kraw, a["kernel"])
                with nc.allow_non_contiguous_dma("short vectors, once"):
                    for at, width, name in ((QGB, 3, "qkv_b"), (PROJB, 1, "proj_b"), (GNW, 1, "gn_w"), (GNB, 1, "gn_b"),
                                            (QB, 3, "in_b"), (LN1B, 1, "ln1_b"), (FFNB, 1, "ffn_b"), (B1, FT, "b1"),
                                            (LN1G, 1, "ln1_g")):
                        load(cols[:, at:at + width], a[name].rearrange("(t p) -> p t", p=P))
                    load(col(S_IN), a["s_in"].partition_broadcast(P))
                    load(col(S_K), a["s_k"].partition_broadcast(P))
                for at, name in ((BO, "out_b"), (RG1, "ln1_g"), (RB1, "ln1_b"), (RB2, "b2"), (RG2, "ln2_g"),
                                 (RBL2, "ln2_b"), (PROJR, "proj_b")):
                    load(rows[:, at, :], a[name].partition_broadcast(P))

            def place_keys(kind, img, h):
                sp.wait_ge(s["k_hi"], upto(2 * img + h))
                sp.wait_ge(s["k_lo"], upto(2 * img + h))
                for head in range(HEADS):
                    mine = slice(HD * head, HD * (head + 1))
                    sp.dma_start(kbd[mine, h, head, :, :], kk[mine, h, :, :]).then_inc(s[f"keys_in{h}"], 16)

            def place_probs(pair):
                def step(kind, img, h):
                    sp.wait_ge(s["pt_hi"], upto(2 * img + h, pair + 1, per=2))
                    sp.wait_ge(s["pt_lo"], upto(2 * img + h, pair + 1, per=2))
                    for w in range(4):
                        mine = slice(WIN * w, WIN * (w + 1))
                        sp.dma_start(ptbd[mine, h, 2 * pair:2 * pair + 2, w, :, :],
                                     pt[mine, h, pair, :, :, :]).then_inc(s[f"probs_in{h}{pair}"], 16)
                return step

            run(sp, "sp", {"k": place_keys, "place0": place_probs(0), "place1": place_probs(1)}, prologue)
            for h in range(2):
                sp.wait_ge(s[f"stored{h}"], 16 * images)

        @block.gpsimd
        def _(pool):
            g = nc.gpsimd

            def prologue():
                for tile, value in ((identf, 0.0), (identh, 0.0), (sel, 0.0), (group_mean, 1.0 / GROUP), (halfpow, -0.5)):
                    g.memset(tile[:], value).then_inc(s["const_made"], 1)
                pool.wait_ge(s["const_made"], 5)
                for tile in (identf, identh):
                    g.affine_select(out=tile[:], in_=tile[:], compare_op=ALU.not_equal, fill=1.0, base=0,
                                    pattern=[[-1, P]], channel_multiplier=1).then_inc(s["const_mask"], 1)
                gm = group_mean[:].rearrange("p (a b) -> p a b", b=GROUP)
                g.affine_select(out=gm, in_=gm, compare_op=ALU.is_ge, fill=0.0, base=0,
                                pattern=[[-GROUP, P // GROUP], [0, GROUP]], channel_multiplier=1).then_inc(s["const_mask"], 1)
                g.affine_select(out=sel[:], in_=sel[:], compare_op=ALU.not_equal, fill=1.0, base=0,
                                pattern=[[-1, HT], [0, P]], channel_multiplier=1).then_inc(s["const_mask"], 1)
                pool.wait_ge(s["const_mask"], 4)
                g.affine_select(out=gm, in_=gm, compare_op=ALU.is_ge, fill=0.0, base=GROUP - 1,
                                pattern=[[GROUP, P // GROUP], [0, GROUP]], channel_multiplier=-1).then_inc(s["const_mask"], 1)
                g.affine_select(out=sel[:], in_=sel[:], compare_op=ALU.not_equal, fill=1.0, base=-HT,
                                pattern=[[-1, HT], [0, P]], channel_multiplier=1).then_inc(s["const_mask"], 1)
                for tile, value in ((cparts[:], 0.0), (minus1[:], -1.0), (vgh[:], 1.0), (ones, 1.0), (ones16[:], 1.0), (shift[:], 0.0)):
                    g.memset(tile, value).then_inc(s["const_made"], 1)
                gn2(None, 0, 0)
                for tile in (vh, vl, kbd, ptbd):
                    g.memset(tile[:], 0.0).then_inc(s["const_made"], 1)

            def gn2(kind, img, _):
                pool.wait_ge(s["gn_veps"], upto(img))
                g.tensor_tensor(gt(GRSTD), gt(GEPS), halfpow[:, 0:1], ALU.pow).then_inc(s["gn_pow"], 1)
                pool.wait_ge(s["h32_made"], upto(img))
                pool.wait_ge(s["h_hi"], upto(img))
                if due(value := upto(img - 1, 2, per=2)):
                    pool.wait_ge(s["vg_mm"], value)
                g.tensor_tensor(hl[:], h32[:], hh[:], ALU.subtract).then_inc(s["h_lo"], 1)

            def st(kind, img, c):
                pool.wait_ge(s[f"p_hi{c % 2}"], upto(img, c // 2 + 1, per=MT))
                pool.wait_ge(s["p_made"], upto(img, c + 1, per=2 * MT))
                if due(value := upto(img, c + 1 - PRING, per=2 * MT)):
                    pool.wait_ge(s["pv_mm"], value)
                g.tensor_tensor(pl[:, c % PRING, :], p32[:, c % PRING, :], ph[:, c % PRING, :],
                                ALU.subtract).then_inc(s["p_lo"], 1)

            def power(n, k, h):
                pool.wait_ge(s[f"ln_veps{k}"], upto(n))
                g.tensor_tensor(rstd[:, h, :], veps[:, h, :], halfpow[:], ALU.pow).then_inc(s[f"ln_pow{k}"], 1)
                pool.wait_ge(s[f"ln_pow{k}"], upto(n))
                if k == 3:
                    g.tensor_tensor(rstd[:, h, :], rstd[:, h, :], col(R_IN).to_broadcast([P, HT]), ALU.mult).then_inc(s["scaled"], 1)
                    pool.wait_ge(s["scaled"], upto(n))
                g.tensor_tensor(nshift[:, h, :], nmean[:, h, :], rstd[:, h, :], ALU.mult).then_inc(s[f"ln_shift{k}"], 1)

            def power_step(k):
                def step(kind, img, h):
                    power(2 * img + h, k, h)
                return step

            def place_lo(pair):
                def step(kind, img, h):
                    n = 2 * img + h
                    pool.wait_ge(s["pt_hi"], upto(n, pair + 1, per=2))
                    if due(value := upto(img - 1, 4, per=4, step=16)):
                        pool.wait_ge(s[f"probs_in{h}{pair}"], value)
                    g.tensor_tensor(pt[:, h, pair, :, 1, :], et[:, h, :].rearrange("p (a b) -> p a b", a=2), pt[:, h, pair, :, 0, :],
                                    ALU.subtract).then_inc(s["pt_lo"], 1)
                return step

            def norm_mid(kind, img, h):
                n = 2 * img + h
                pool.wait_ge(s["norm_made1"], upto(n))
                g.tensor_tensor(res[:, h], y[:, h], row(RG1), ALU.mult).then_inc(s["r1_made"], 1)

            def up(f):
                def step(kind, img, h):
                    n = 2 * img + h
                    pool.wait_ge(s["hid_hi"], upto(n, f + 1, per=FT))
                    pool.wait_ge(s["hid_made"], upto(n, f + 1, per=FT))
                    if due(value := upto(n - 1)):
                        pool.wait_ge(s["down_mm"], value)
                    g.tensor_tensor(fl[:, f, :], hid[:, f % 2, :], fh[:, f, :], ALU.subtract).then_inc(s["hid_lo"], 1)
                return step

            def norm_out(kind, img, h):
                n = 2 * img + h
                g.tensor_tensor(t[:, h], t[:, h], row(RBL2), ALU.add).then_inc(s["t2b_made"], 1)
                pool.wait_ge(s["norm_made2"], upto(n))
                g.tensor_tensor(y[:, h], y[:, h], row(RG2), ALU.mult).then_inc(s["t2a_made"], 1)
                pool.wait_ge(s["t2a_made"], upto(n))
                pool.wait_ge(s["t2b_made"], upto(n))
                g.tensor_tensor(t[:, h], t[:, h], y[:, h], ALU.add).then_inc(s["t2_made"], 1)

            run(pool, "pool", {"gn2": gn2, "st": st, "ln_in": power_step(0), "place0": place_lo(0),
                       "place1": place_lo(1), "out": power_step(1), "norm_mid": norm_mid, "up0": up(0), "up1": up(1),
                       "up2": up(2), "up3": up(3), "down": power_step(2), "norm_out": norm_out,
                       "ln_q": power_step(3)}, prologue)

        @block.scalar
        def _(act):
            sc = nc.scalar

            def prologue():
                gn2(None, 0, 0)

            def gn2(kind, img, _):
                act.wait_ge(s["gn_coef"], upto(img))
                act.wait_ge(s["x_in"], upto(img, step=16))
                if due(value := upto(img - 1, 2, per=2)):
                    act.wait_ge(s["vg_mm"], value)
                sc.activation(hh[:], x_sb[:], ACT.Identity, bias=gt(GBIAS), scale=gt(GSCALE)).then_inc(s["h_hi"], 1)

            def load_x(kind, img, _):
                if due(value := upto(img - 1, 2, per=2)):
                    act.wait_ge(s["turn_x_mm"], value)
                if due(value := upto(img - 1)):
                    act.wait_ge(s["h_hi"], value)
                if due(value := upto(img - 1)):
                    act.wait_ge(s["h32_made"], value)
                act.dma_start(x_sb[:, :], a["x"][img]).then_inc(s["x_in"], 16)

            def normalise(dst, src, k):
                def step(kind, img, h):
                    act.wait_ge(s[f"ln_shift{k}"], upto(2 * img + h))
                    for j in range(HT):
                        last = sc.activation(dst[:, h, P * j:P * (j + 1)] if dst is z else dst[:, h, j, :], src[:, h, j, :],
                                             ACT.Identity, bias=nshift[:, h, j:j + 1], scale=rstd[:, h, j:j + 1])
                    last.then_inc(s[f"norm_made{k}"], 1)
                return step

            def global_hi(name, dst, bias):
                def step(kind, img, c):
                    act.wait_ge(s[name + "_mm"], upto(img, c + 1, per=2))
                    sc.activation(dst[:, HALF * c:HALF * (c + 1)], bank(name, c), ACT.Identity,
                                  bias=col(bias)).then_inc(s[name + "_hi"], 1)
                return step

            def vg(kind, img, c):
                act.wait_ge(s["vg_mm"], upto(img, c + 1, per=2))
                if isinstance(img, int) and img == 0 and c == 0:
                    act.wait_ge(s["const_made"], 11)
                sc.activation(vgh[:, HT * c:HT * (c + 1), 0:C], tiles(bank("vg", c)), ACT.Copy).then_inc(s["vg_hi"], 1)

            def st(kind, img, c):
                act.wait_ge(s["st_mm"], upto(img, c + 1, per=2 * MT))
                if c % 2 == 0:
                    if due(value := upto(img, c + 1 - PRING, per=2 * MT)):
                        act.wait_ge(s["pv_mm"], value)
                    sc.activation(ph[:, c % PRING, :], bank("st", c), ACT.Exp, scale=C ** -0.5).then_inc(s["p_hi0"], 1)
                if due(value := upto(img, c + 1 - PRING, per=2 * MT)):
                    act.wait_ge(s["p_lo"], value)
                sc.activation(p32[:, c % PRING, :], bank("st", c), ACT.Exp, scale=C ** -0.5).then_inc(s["p_made"], 1)

            def turned_hi(name, signal):
                def step(kind, img, h):
                    n = 2 * img + h
                    act.wait_ge(s[name + "_mm"], upto(n))
                    sc.activation(xh[:, h, :], bank(name, h), ACT.Copy).then_inc(s[signal], 1)
                return step

            def q(kind, img, h):
                act.wait_ge(s["q_mm"], upto(2 * img + h))
                sc.activation(qh[:, h, :], bank("q", h), ACT.Identity, bias=col(QB)).then_inc(s["q_hi"], 1)

            def k(kind, img, h):
                n = 2 * img + h
                act.wait_ge(s["k_mm"], upto(n))
                if due(value := upto(img - 1, HEADS, per=HEADS, step=16)):
                    act.wait_ge(s[f"keys_in{h}"], value)
                sc.activation(kk[:, h, 0, :], bank("k", h), ACT.Identity, bias=col(KB)).then_inc(s["k_hi"], 1)

            def v(kind, img, h):
                n = 2 * img + h
                act.wait_ge(s["v_mm"], upto(n))
                if isinstance(img, int) and img == 0:
                    act.wait_ge(s["const_made"], 15)
                src = bank("v", h).rearrange("p (b c) -> p b c", c=2 * HD)
                for odd in range(2):
                    mine = slice(HD * odd, HD * (odd + 1))
                    dst = vh[:, h, odd].rearrange("p a (b c) -> p (a b) c", c=2 * HD)
                    last = sc.activation(dst[:, :, mine], src[:, :, mine], ACT.Copy)
                last.then_inc(s["v_hi"], 1)

            def score(pair):
                def step(kind, img, h):
                    act.wait_ge(s["sub_made"], upto(2 * img + h, pair + 1, per=2))
                    sc.activation(e[:, h, :], e[:, h, :], ACT.Exp, scale=HD ** -0.5).then_inc(s["exp_made"], 1)
                return step

            def place_hi(pair):
                def step(kind, img, h):
                    n = 2 * img + h
                    act.wait_ge(s["et_made"], upto(n, pair + 1, per=2))
                    if due(value := upto(img - 1, 4, per=4, step=16)):
                        act.wait_ge(s[f"probs_in{h}{pair}"], value)
                    sc.activation(pt[:, h, pair, :, 0, :], et[:, h, :].rearrange("p (a b) -> p a b", a=2), ACT.Copy).then_inc(s["pt_hi"], 1)
                return step

            def pv1(kind, img, h):
                act.wait_ge(s["pv_win_mm"], upto(2 * img + h))
                sc.activation(oh[:, h, :], bank("pv0", h), ACT.Copy).then_inc(s["o_hi"], 1)

            def up(f):
                def step(kind, img, h):
                    n = 2 * img + h
                    act.wait_ge(s["up_mm"], upto(n, f + 1, per=FT))
                    if due(value := upto(n - 1)):
                        act.wait_ge(s["down_mm"], value)
                    sc.activation(fh[:, f, :], bank(f"up{f}", h), ACT.Relu, bias=col(B1F + f)).then_inc(s["hid_hi"], 1)
                    if due(value := upto(n, f + 1 - 2, per=FT)):
                        act.wait_ge(s["hid_lo"], value)
                    sc.activation(hid[:, f % 2, :], bank(f"up{f}", h), ACT.Relu, bias=col(B1F + f)).then_inc(s["hid_made"], 1)
                return step

            def turn_q(kind, img, h):
                act.wait_ge(s["turn_q_mm"], upto(2 * img + h))
                sc.activation(qt[:, h, :], bank("turn_q", h)[:, 0:HALF // 2].bitcast(BF16), ACT.Copy).then_inc(s["qt_made"], 1)

            def ffn(kind, img, h):
                n = 2 * img + h
                act.wait_ge(s["ffn_mm"], upto(n))
                if due(value := upto(img - 1, step=16)):
                    act.wait_ge(s[f"stored{h}"], value)
                sc.activation(o_sb[:, h, :], bank("ffn", h), ACT.Identity, bias=col(BFB)).then_inc(s["o_made"], 1)
                act.wait_ge(s["o_made"], upto(n))
                act.dma_start(out[img, :, HALF * h:HALF * (h + 1)], o_sb[:, h, :]).then_inc(s[f"stored{h}"], 16)

            run(act, "act", {"norm_in": normalise(y, t, 0), "norm_mid": normalise(y, y, 1), "norm_out": normalise(y, y, 2),
                      "quant": normalise(z, t, 3), "load_x": load_x, "gn2": gn2, "qg": global_hi("qg", qgh, QGB), "kg": global_hi("kg", kgh, KGB), "vg": vg, "st": st,
                      "turn_in": turned_hi("turn_in", "x_hi"), "q": q, "k": k, "v": v, "score0": score(0),
                      "score1": score(1), "place0": place_hi(0), "place1": place_hi(1), "pv1": pv1,
                      "turn_mid": turned_hi("turn_mid", "m_hi"), "up0": up(0), "up1": up(1), "up2": up(2),
                      "up3": up(3), "turn_q": turn_q, "ffn": ffn}, prologue)

        @block.vector
        def _(dve):
            v_ = nc.vector
            setup = [0]

            def link(ins):
                setup[0] += 1
                ins.then_inc(s["setup_dve"], 1)
                dve.wait_ge(s["setup_dve"], setup[0])

            def prologue():
                gn0(None, 0, 0)
                dve.wait_ge(s["weights_in"], 16 * 26)
                dve.wait_ge(s["const_made"], 11)
                dve.wait_ge(s["const_mask"], 6)
                link(v_.tensor_scalar(vb_full[:, 0, :], ones, col(VGB), None, ALU.mult))
                link(v_.tensor_scalar(vb_full[:, 1, :], ones, col(VB), None, ALU.mult))
                gn1(None, 0, 0)
                gn2(None, 0, 0)
                dve.wait_ge(s["setup_mm"], 1)
                for w in (QG, KG, Q, K, V, OUT):
                    link(v_.tensor_copy(wh[:, w, :], wraw[:, w, :]))
                    link(v_.tensor_tensor(wl[:, w, :], wraw[:, w, :], wh[:, w, :], ALU.subtract))
                link(v_.tensor_copy(wh[:, PVG, :], ps[:, 3, 0:P]))
                link(v_.tensor_tensor(wl[:, PVG, :], ps[:, 3, 0:P], wh[:, PVG, :], ALU.subtract))
                link(v_.tensor_tensor(rows[:, PROJR, :], ps[:, 4, 0:P], rows[:, PROJR, :], ALU.add))
                link(v_.tensor_tensor(rows[:, BO, :], ps[:, 4, P:2 * P], rows[:, BO, :], ALU.add))
                link(v_.tensor_tensor(cols[:, B1F:B1F + FT], ps[:, 5, 0:FT], cols[:, B1:B1 + FT], ALU.add))
                link(v_.tensor_tensor(rows[:, RB1, :], rows[:, RB1, :], rows[:, RB2, :], ALU.add))
                for b, r in ((BIAS_OUT, BO), (BIAS_DOWN, RB1)):
                    link(v_.memset(bias16[:, b, :], 0.0))
                    for k in range(3):
                        link(v_.tensor_copy(part16, rows[:, r, :]))
                        link(v_.tensor_tensor(rows[:, r, :], rows[:, r, :], part16, ALU.subtract))
                        link(v_.scalar_tensor_tensor(bias16[:, b, :], part16, identf[:, k:k + 1], bias16[:, b, :],
                                                     ALU.mult, ALU.add))
                link(v_.tensor_scalar(w1raw, w1raw, col(LN1G), None, ALU.mult))
                for raw, hi, lo in ((w1raw, w1h, w1l), (w2raw, w2h, w2l)):
                    link(v_.tensor_copy(hi[:], raw))
                    link(v_.tensor_tensor(lo[:], raw, hi[:], ALU.subtract))
                link(v_.tensor_copy(ffnb16[:], col(FFNB)))
                link(v_.tensor_copy(col(BFB), ffnb16[:]))
                link(v_.reciprocal(col(R_IN), col(S_IN)))
                link(v_.reciprocal(col(R_K), col(S_K)))
                link(v_.tensor_tensor(col(S_BOTH), col(S_IN), col(S_K), ALU.mult))
                link(v_.tensor_scalar(kraw, kraw, col(R_K), None, ALU.mult))
                link(v_.tensor_scalar(kraw, kraw, E4M3_MAX, -E4M3_MAX, ALU.min, ALU.max))
                link(v_.tensor_scalar(expo[:, 0:P].bitcast(I32), kraw.bitcast(I32), EXP_MASK, None, ALU.bitwise_and))
                link(v_.tensor_scalar(expo[:, 0:P], expo[:, 0:P], E4M3_MIN_NORMAL, None, ALU.max))
                link(v_.scalar_tensor_tensor(kraw, expo[:, 0:P], ROUND_3_BITS, kraw, ALU.mult, ALU.add))
                link(v_.scalar_tensor_tensor(kraw, expo[:, 0:P], -ROUND_3_BITS, kraw, ALU.mult, ALU.add))
                link(v_.tensor_scalar(kraw, kraw, col(S_BOTH), None, ALU.mult))
                link(v_.tensor_copy(kh[:], kraw))
                link(v_.tensor_tensor(kl[:], kraw, kh[:], ALU.subtract))

            def gn0(kind, img, _):
                dve.wait_ge(s["x_in"], upto(img, step=16))
                v_.bn_stats(gst[:, 0, :], x_sb[:, 0:HALF])
                v_.bn_stats(gst[:, 1, :], x_sb[:, HALF:N]).then_inc(s["gn_stats"], 1)
                dve.wait_ge(s["gn_stats"], upto(img))
                v_.memset(spare[:], 0.0)
                v_.bn_aggr(gmv[:], gst[:].rearrange("p a b -> p (a b)")).then_inc(s["gn_mv"], 1)

            def gn1(kind, img, _):
                dve.wait_ge(s["gn_mm"], upto(img, 1, per=2))
                v_.tensor_copy(gt(GMEAN), bank("gn1", 0)[:, 0:1]).then_inc(s["gn_mean"], 1)
                dve.wait_ge(s["gn_mean"], upto(img))
                v_.tensor_tensor(gt(GDIFF), gmv[:, 0:1], gt(GMEAN), ALU.subtract).then_inc(s["gn_diff"], 1)
                dve.wait_ge(s["gn_diff"], upto(img))
                v_.scalar_tensor_tensor(gt(GVAR), gt(GDIFF), gt(GDIFF), gmv[:, 1:2], ALU.mult, ALU.add).then_inc(s["gn_var"], 1)

            def gn2(kind, img, _):
                dve.wait_ge(s["gn_mm"], upto(img, 2, per=2))
                v_.tensor_scalar(gt(GEPS), bank("gn2", 0)[:, 0:1], EPS, None, ALU.add).then_inc(s["gn_veps"], 1)
                dve.wait_ge(s["gn_pow"], upto(img))
                v_.tensor_tensor(gt(GSCALE), gt(GRSTD), col(GNW), ALU.mult).then_inc(s["gn_scale"], 1)
                dve.wait_ge(s["gn_scale"], upto(img))
                v_.scalar_tensor_tensor(gt(GNEG), gt(GSCALE), gt(GMEAN), col(GNB), ALU.mult, ALU.subtract).then_inc(s["gn_neg"], 1)
                dve.wait_ge(s["gn_neg"], upto(img))
                v_.tensor_scalar(gt(GBIAS), gt(GNEG), -1.0, None, ALU.mult).then_inc(s["gn_coef"], 1)
                dve.wait_ge(s["gn_coef"], upto(img))
                if due(value := upto(img - 1)):
                    dve.wait_ge(s["h_lo"], value)
                v_.tensor_scalar(h32[:], x_sb[:], gt(GSCALE), gt(GBIAS), ALU.mult, ALU.add).then_inc(s["h32_made"], 1)

            def global_lo(name, hi, lo, bias):
                def step(kind, img, c):
                    dve.wait_ge(s[name + "_hi"], upto(img, c + 1, per=2))
                    part = slice(HALF * c, HALF * (c + 1))
                    v_.scalar_tensor_tensor(lo[:, part], bank(name, c), col(bias), hi[:, part], ALU.add,
                                            ALU.subtract).then_inc(s[name + "_lo"], 1)
                return step

            def vg(kind, img, c):
                dve.wait_ge(s["vg_hi"], upto(img, c + 1, per=2))
                part = slice(HT * c, HT * (c + 1))
                v_.tensor_tensor(vgl[:, part, :], tiles(bank("vg", c)), vgh[:, part, 0:C], ALU.subtract).then_inc(s["vg_lo"], 1)

            def turn_x(kind, img, c):
                dve.wait_ge(s["turn_x_mm"], upto(img, c + 1, per=2))
                v_.tensor_tensor(xt[:, c], tiles(bank("turn_x", c)), row(PROJR), ALU.add).then_inc(s["xt_made"], 1)

            def row_max(kind, img, c):
                dve.wait_ge(s["max_mm"], upto(img, c + 1, per=2 * MT))
                v_.reduce_max(cm[:, c // 2, c % 2:c % 2 + 1], bank("max", c), X).then_inc(s["max_out"], 1)

            def maxima(kind, img, c):
                dve.wait_ge(s["max_out"], upto(img, MT * (c + 1), per=2 * MT))
                v_.reduce_max(cmax[:], cm[:, HT * c:HT * (c + 1), :], X).then_inc(s["cmax_made"], 1)
                dve.wait_ge(s["cmax_made"], upto(img, c + 1, per=2))
                v_.tensor_copy(chi[:], cmax[:]).then_inc(s["chi_made"], 1)
                dve.wait_ge(s["chi_made"], upto(img, c + 1, per=2))
                if due(value := upto(img, c, per=2)):
                    dve.wait_ge(s["shift_turned"], value)
                v_.tensor_copy(cparts[:, 0:HT], chi[:])
                v_.tensor_tensor(cparts[:, HT:2 * HT], cmax[:], chi[:], ALU.subtract).then_inc(s["cparts_made"], 1)

            def make_shift(kind, img, c):
                dve.wait_ge(s["shift_turned"], upto(img, c + 1, per=2))
                turned = ps[0:2 * HT, BANK["shift", c]:BANK["shift", c] + 1, 0:P].to_broadcast([2 * HT, HT, P])
                v_.tensor_tensor(shift[0:2 * HT, c], turned, sel[:], ALU.mult).then_inc(s["shift_made"], 1)

            def st(kind, img, c):
                if c % 2 == 0:
                    return
                dve.wait_ge(s["p_made"], upto(img, c + 1, per=2 * MT))
                if due(value := upto(img, c + 1 - PRING, per=2 * MT)):
                    dve.wait_ge(s["pv_mm"], value)
                v_.tensor_copy(ph[:, c % PRING, :], p32[:, c % PRING, :]).then_inc(s["p_hi1"], 1)

            def pv(kind, img, c):
                if c % MT != MT - 1:
                    return
                h = c // MT
                dve.wait_ge(s["pv_mm"], upto(img, c + 1, per=2 * MT))
                acc = ps[:, PV_BANKS[0]:PV_BANKS[1] + 1, 0:2 * PVW].rearrange("p a (b c) -> p a b c", c=PVW)
                v_.reciprocal(rsum[:], acc[:, :, :, C]).then_inc(s["rsum_made"], 1)
                dve.wait_ge(s["rsum_made"], upto(img, h + 1, per=2))
                dve.wait_ge(s["xt_made"], upto(img, 2, per=2))
                if due(value := upto(2 * img + h - 2)):
                    dve.wait_ge(s["ffn_mm"], value)
                for j in range(HT):
                    last = v_.scalar_tensor_tensor(t[:, h, j, :], acc[:, j // 2, j % 2, 0:C], rsum[:, j // 2, j % 2:j % 2 + 1],
                                                   xt[:, h, j, :], ALU.mult, ALU.add)
                last.then_inc(s["t_made"], 1)

            def variance(src, n, k, h):
                for j in range(HT):
                    last = v_.bn_stats(stats[:, h, j, :], src[:, h, j, :])
                last.then_inc(s[f"ln_stats{k}"], 1)
                dve.wait_ge(s[f"ln_stats{k}"], upto(n))
                v_.memset(spare[:], 0.0)
                for j in range(HT):
                    last = v_.bn_aggr(mv[:, h, j, :], stats[:, h, j, :])
                last.then_inc(s[f"ln_mv{k}"], 1)
                dve.wait_ge(s[f"ln_mv{k}"], upto(n))
                v_.tensor_scalar(nmean[:, h, :], mv[:, h, :, 0], -1.0, None, ALU.mult)
                v_.tensor_scalar(veps[:, h, :], mv[:, h, :, 1], EPS, None, ALU.add).then_inc(s[f"ln_veps{k}"], 1)

            def ln_in(kind, img, h):
                dve.wait_ge(s["t_made"], upto(2 * img + h))
                variance(t, 2 * img + h, 0, h)

            def turned_lo(name, hi_signal, signal):
                def step(kind, img, h):
                    dve.wait_ge(s[hi_signal], upto(2 * img + h))
                    v_.tensor_tensor(xl[:, h, :], bank(name, h), xh[:, h, :], ALU.subtract).then_inc(s[signal], 1)
                return step

            def q(kind, img, h):
                dve.wait_ge(s["q_hi"], upto(2 * img + h))
                v_.scalar_tensor_tensor(ql[:, h, :], bank("q", h), col(QB), qh[:, h, :], ALU.add,
                                        ALU.subtract).then_inc(s["q_lo"], 1)

            def k(kind, img, h):
                n = 2 * img + h
                dve.wait_ge(s["k_hi"], upto(n))
                if due(value := upto(img - 1, HEADS, per=HEADS, step=16)):
                    dve.wait_ge(s[f"keys_in{h}"], value)
                v_.scalar_tensor_tensor(kk[:, h, 1, :], bank("k", h), col(KB), kk[:, h, 0, :], ALU.add,
                                        ALU.subtract).then_inc(s["k_lo"], 1)

            def v(kind, img, h):
                dve.wait_ge(s["v_hi"], upto(2 * img + h))
                src = bank("v", h).rearrange("p (b c) -> p b c", c=2 * HD)
                for odd in range(2):
                    mine = slice(HD * odd, HD * (odd + 1))
                    hi = vh[:, h, odd].rearrange("p a (b c) -> p (a b) c", c=2 * HD)
                    lo = vl[:, h, odd].rearrange("p a (b c) -> p (a b) c", c=2 * HD)
                    last = v_.tensor_tensor(lo[:, :, mine], src[:, :, mine], hi[:, :, mine], ALU.subtract)
                last.then_inc(s["v_lo"], 1)

            def by_head(ap):
                return ap.rearrange("p (a b) -> p a b", b=WIN)

            def spread(ap):
                return ap.unsqueeze(2).to_broadcast([P, 2 * HEADS, WIN])

            def score(pair):
                def step(kind, img, h):
                    n = 2 * img + h
                    dve.wait_ge(s["score_mm"], upto(n, pair + 1, per=2))
                    v_.reduce_max(smax[:, h, :], by_head(bank(f"score{pair}", h)), X).then_inc(s["smax_made"], 1)
                    dve.wait_ge(s["smax_made"], upto(n, pair + 1, per=2))
                    v_.tensor_tensor(by_head(e[:, h, :]), by_head(bank(f"score{pair}", h)), spread(smax[:, h, :]),
                                     ALU.subtract).then_inc(s["sub_made"], 1)
                return step

            def prob(pair):
                def step(kind, img, h):
                    n = 2 * img + h
                    dve.wait_ge(s["exp_made"], upto(n, pair + 1, per=2))
                    v_.reduce_sum(ssum[:, h, :], by_head(e[:, h, :]), X).then_inc(s["ssum_made"], 1)
                    dve.wait_ge(s["ssum_made"], upto(n, pair + 1, per=2))
                    v_.reciprocal(srec[:, h, :], ssum[:, h, :]).then_inc(s["srec_made"], 1)
                    dve.wait_ge(s["srec_made"], upto(n, pair + 1, per=2))
                    v_.tensor_tensor(by_head(e[:, h, :]), by_head(e[:, h, :]), spread(srec[:, h, :]),
                                     ALU.mult).then_inc(s["prob_made"], 1)
                    dve.wait_ge(s["prob_made"], upto(n, pair + 1, per=2))
                    if pair:
                        dve.wait_ge(s["pt_lo"], upto(n, 1, per=2))
                    v_.transpose(et[:, h, :], e[:, h, :]).then_inc(s["et_made"], 1)
                return step

            def pv1(kind, img, h):
                dve.wait_ge(s["o_hi"], upto(2 * img + h))
                v_.tensor_tensor(ol[:, h, :], bank("pv0", h), oh[:, h, :], ALU.subtract).then_inc(s["o_lo"], 1)

            def out_proj(kind, img, h):
                n = 2 * img + h
                dve.wait_ge(s["out_mm"], upto(n))
                v_.tensor_tensor(y[:, h], tiles(bank("out", h)), y[:, h], ALU.add).then_inc(s["y1_made"], 1)
                dve.wait_ge(s["y1_made"], upto(n))
                variance(y, n, 1, h)

            def down(kind, img, h):
                n = 2 * img + h
                dve.wait_ge(s["down_mm"], upto(n))
                dve.wait_ge(s["r1_made"], upto(n))
                v_.tensor_tensor(y[:, h], tiles(bank("down", h)), res[:, h], ALU.add).then_inc(s["y2_made"], 1)
                dve.wait_ge(s["y2_made"], upto(n))
                variance(y, n, 2, h)

            def ln_q(kind, img, h):
                dve.wait_ge(s["t2_made"], upto(2 * img + h))
                variance(t, 2 * img + h, 3, h)

            def quant(kind, img, h):
                n = 2 * img + h
                dve.wait_ge(s["norm_made3"], upto(n))
                v_.tensor_scalar(z[:, h], z[:, h], E4M3_MAX, -E4M3_MAX, ALU.min, ALU.max).then_inc(s["clipped"], 1)
                dve.wait_ge(s["clipped"], upto(n))
                v_.tensor_scalar(expo[:].bitcast(I32), z[:, h].bitcast(I32), EXP_MASK, None, ALU.bitwise_and).then_inc(s["expo_made"], 1)
                dve.wait_ge(s["expo_made"], upto(n))
                v_.tensor_scalar(expo[:], expo[:], E4M3_MIN_NORMAL, None, ALU.max).then_inc(s["expo_low"], 1)
                dve.wait_ge(s["expo_low"], upto(n))
                v_.scalar_tensor_tensor(z[:, h], expo[:], ROUND_3_BITS, z[:, h], ALU.mult, ALU.add).then_inc(s["rounded"], 1)
                dve.wait_ge(s["rounded"], upto(n))
                v_.scalar_tensor_tensor(qz[:, h].rearrange("p a b -> p (a b)"), expo[:], -ROUND_3_BITS, z[:, h], ALU.mult,
                                        ALU.add).then_inc(s["qz_made"], 1)

            run(dve, "dve", {"gn0": gn0, "gn1": gn1, "gn2": gn2, "qg": global_lo("qg", qgh, qgl, QGB),
                      "kg": global_lo("kg", kgh, kgl, KGB), "vg": vg, "turn_x": turn_x, "max": row_max,
                      "maxima": maxima, "shift": make_shift, "st": st, "pv": pv, "ln_in": ln_in,
                      "turn_in": turned_lo("turn_in", "x_hi", "x_lo"), "q": q, "k": k, "v": v, "score0": score(0),
                      "score1": score(1), "prob0": prob(0), "prob1": prob(1), "pv1": pv1, "out": out_proj,
                      "turn_mid": turned_lo("turn_mid", "m_hi", "m_lo"), "down": down, "ln_q": ln_q,
                      "quant": quant}, prologue)

        @block.tensor
        def _(pe):
            mm = nc.tensor.matmul

            def claim(kind, img, name, index):
                if (kind, name, index) not in before:
                    return
                pname, pindex, back = before[kind, name, index]
                signal, per, by_half = RELEASE[pname]
                if by_half:
                    k = int(pname[-1]) + 1 if per > 1 else 1
                    pe.wait_ge(s[signal], upto(2 * (img - back) + pindex, k, per=per))
                else:
                    pe.wait_ge(s[signal], upto(img - back, pindex + 1, per=per))

            def bias_first(dst, b):
                mm(tiles(dst), ones16[:], bias16[:, b:b + 1, :].to_broadcast([P, HT, P]), start=True, stop=False)

            def three(dst, lhi, llo, rhi, rlo, first=True, last=True, **kw):
                mm(dst, lhi, rhi, start=first, stop=False, **kw)
                mm(dst, lhi, rlo, start=False, stop=False, **kw)
                return mm(dst, llo, rhi, start=False, stop=last, **kw)

            def prologue():
                gn1(None, 0, 0)
                pe.wait_ge(s["weights_in"], 16 * 26)
                pe.wait_ge(s["setup_dve"], 2)
                mm(ps[:, 3, 0:P], wraw[:, VG, :], wraw[:, PROJ, :], start=True, stop=True)
                mm(ps[:, 4, 0:P], vb_full[:, 0, :], wraw[:, PROJ, :], start=True, stop=True)
                mm(ps[:, 4, P:2 * P], vb_full[:, 1, :], wraw[:, OUT, :], start=True, stop=True)
                for f in range(FT):
                    last = mm(ps[:, 5, f:f + 1], w1raw[:, P * f:P * (f + 1)], col(LN1B), start=True, stop=True)
                last.then_inc(s["setup_mm"], 1)
                gn2(None, 0, 0)
                pe.wait_ge(s["setup_dve"], SETUP_STEPS)

            def gn1(kind, img, _):
                claim(kind or "prologue", img, "gn1", 0)
                if kind is None:
                    pe.wait_ge(s["const_mask"], 6)
                pe.wait_ge(s["gn_mv"], upto(img))
                mm(bank("gn1", 0)[:, 0:1], group_mean[:], gmv[:, 0:1], start=True, stop=True).then_inc(s["gn_mm"], 1)

            def gn2(kind, img, _):
                claim(kind or "prologue", img, "gn2", 0)
                pe.wait_ge(s["gn_var"], upto(img))
                mm(bank("gn2", 0)[:, 0:1], group_mean[:], gt(GVAR), start=True, stop=True).then_inc(s["gn_mm"], 1)

            def project(name, w):
                def step(kind, img, c):
                    claim(kind, img, name, c)
                    pe.wait_ge(s["h_hi"], upto(img))
                    pe.wait_ge(s["h_lo"], upto(img))
                    part = slice(HALF * c, HALF * (c + 1))
                    three(bank(name, c), wh[:, w, :], wl[:, w, :], hh[:, part], hl[:, part]).then_inc(s[name + "_mm"], 1)
                return step

            def vg(kind, img, c):
                claim(kind, img, "vg", c)
                pe.wait_ge(s["h_lo"], upto(img))
                for j in range(HT):
                    part = slice(HALF * c + P * j, HALF * c + P * (j + 1))
                    last = three(bank("vg", c)[:, P * j:P * (j + 1)], hh[:, part], hl[:, part], wh[:, PVG, :], wl[:, PVG, :])
                last.then_inc(s["vg_mm"], 1)

            def turn_x(kind, img, c):
                claim(kind, img, "turn_x", c)
                for j in range(HT):
                    part = slice(HALF * c + P * j, HALF * c + P * (j + 1))
                    last = nc.tensor.transpose(bank("turn_x", c)[:, P * j:P * (j + 1)], x_sb[:, part], identf[:])
                last.then_inc(s["turn_x_mm"], 1)

            def row_max(kind, img, c):
                claim(kind, img, "max", c)
                pe.wait_ge(s["qg_hi"], upto(img, c // MT + 1, per=2))
                pe.wait_ge(s["kg_hi"], upto(img, c % 2 + 1, per=2))
                mm(bank("max", c), qgh[:, P * (c // 2):P * (c // 2 + 1)], kgh[:, HALF * (c % 2):HALF * (c % 2 + 1)],
                   start=True, stop=True).then_inc(s["max_mm"], 1)

            def turn_shift(kind, img, c):
                claim(kind, img, "shift", c)
                pe.wait_ge(s["cparts_made"], upto(img, c + 1, per=2))
                nc.tensor.transpose(bank("shift", c)[:, 0:P], cparts[:], identf[:]).then_inc(s["shift_turned"], 1)

            def st(kind, img, c):
                h, j = divmod(c, MT)
                claim(kind, img, "st", c)
                pe.wait_ge(s["shift_made"], upto(img, h + 1, per=2))
                pe.wait_ge(s["qg_lo"], upto(img, h + 1, per=2))
                pe.wait_ge(s["kg_lo"], upto(img, j // HT + 1, per=2))
                keys, queries = slice(P * j, P * (j + 1)), slice(HALF * h, HALF * (h + 1))
                mm(bank("st", c), minus1[:], shift[:, h].rearrange("p a b -> p (a b)"), start=True, stop=False)
                three(bank("st", c), kgh[:, keys], kgl[:, keys], qgh[:, queries], qgl[:, queries],
                      first=False).then_inc(s["st_mm"], 1)

            def pv(kind, img, c):
                h, j = divmod(c, MT)
                if j == 0:
                    if due(value := upto(2 * img + h - 1)):
                        pe.wait_ge(s["t_made"], value)
                    pe.wait_ge(s["vg_lo"], upto(img, 2, per=2))
                pe.wait_ge(s[f"p_hi{c % 2}"], upto(img, c // 2 + 1, per=MT))
                pe.wait_ge(s["p_lo"], upto(img, c + 1, per=2 * MT))
                for q in range(HT):
                    b, at = PV_BANKS[q // 2], PVW * (q % 2)
                    part = slice(P * q, P * (q + 1))
                    mm(ps[:, b, at:at + PVW], ph[:, c % PRING, part], vgh[:, j, :], start=j == 0 and q % 2 == 0,
                       stop=False, skip_group_check=True)
                    mm(ps[:, b, at:at + C], ph[:, c % PRING, part], vgl[:, j, :], start=False, stop=False,
                       skip_group_check=True)
                    last = mm(ps[:, b, at:at + PVW], pl[:, c % PRING, part], vgh[:, j, :], start=False,
                              stop=j == MT - 1, skip_group_check=True)
                last.then_inc(s["pv_mm"], 1)

            def turn(name, src, k):
                def step(kind, img, h):
                    n = 2 * img + h
                    claim(kind, img, name, h)
                    pe.wait_ge(s[f"norm_made{k}"], upto(n))
                    for j in range(HT):
                        last = nc.tensor.transpose(bank(name, h)[:, P * j:P * (j + 1)], src[:, h, j, :], identf[:])
                    last.then_inc(s[name + "_mm"], 1)
                return step

            def q(kind, img, h):
                claim(kind, img, "q", h)
                pe.wait_ge(s["x_lo"], upto(2 * img + h))
                three(bank("q", h), wh[:, Q, :], wl[:, Q, :], xh[:, h, :], xl[:, h, :]).then_inc(s["q_mm"], 1)

            def k(kind, img, h):
                claim(kind, img, "k", h)
                pe.wait_ge(s["x_lo"], upto(2 * img + h))
                three(bank("k", h), wh[:, K, :], wl[:, K, :], xh[:, h, :], xl[:, h, :]).then_inc(s["k_mm"], 1)

            def v(kind, img, h):
                claim(kind, img, "v", h)
                pe.wait_ge(s["x_lo"], upto(2 * img + h))
                for j in range(HT):
                    part = slice(P * j, P * (j + 1))
                    last = three(bank("v", h)[:, part], xh[:, h, part], xl[:, h, part], wh[:, V, :], wl[:, V, :])
                last.then_inc(s["v_mm"], 1)

            def score(pair):
                def step(kind, img, h):
                    n = 2 * img + h
                    name = f"score{pair}"
                    claim(kind, img, name, h)
                    pe.wait_ge(s["q_lo"], upto(n))
                    pe.wait_ge(s[f"keys_in{h}"], upto(img, HEADS, per=HEADS, step=16))
                    for tt in range(2):
                        for m, (left, part) in enumerate(((qh, 0), (qh, 1), (ql, 0))):
                            for w in range(4):
                                tok = P * (2 * pair + tt) + WIN * w
                                last = mm(ps[WIN * w:WIN * (w + 1), BANK[name, h], HALF // 2 * tt:HALF // 2 * (tt + 1)],
                                          left[:, h, tok:tok + WIN], kbd[:, h, :, part, tok:tok + WIN],
                                          start=m == 0, stop=m == 2)
                    last.then_inc(s["score_mm"], 1)
                return step

            def pv_win(pair):
                def step(kind, img, h):
                    n = 2 * img + h
                    if pair == 0:
                        claim(kind, img, "pv0", h)
                        pe.wait_ge(s["v_lo"], upto(n))
                    pe.wait_ge(s[f"probs_in{h}{pair}"], upto(img, 4, per=4, step=16))
                    for j in (2 * pair, 2 * pair + 1):
                        for m, (val, part, odd) in enumerate(((vh, 0, 0), (vl, 0, 0), (vh, 1, 0), (vh, 0, 1), (vl, 0, 1), (vh, 1, 1))):
                            for two in range(4):
                                head = 2 * two + odd
                                last = mm(ps[WIN * two:WIN * (two + 1), BANK["pv0", h], P * j:P * (j + 1)],
                                          val[:, h, odd, j, WIN * two:WIN * (two + 1)],
                                          ptbd[:, h, j, :, part, WIN * head:WIN * (head + 1)],
                                          start=m == 0, stop=m == 5)
                    if pair == 1:
                        last.then_inc(s["pv_win_mm"], 1)
                return step

            def out_proj(kind, img, h):
                claim(kind, img, "out", h)
                pe.wait_ge(s["o_lo"], upto(2 * img + h))
                bias_first(bank("out", h), BIAS_OUT)
                for j in range(HT):
                    part = slice(P * j, P * (j + 1))
                    last = three(bank("out", h)[:, part], oh[:, h, part], ol[:, h, part], wh[:, OUT, :], wl[:, OUT, :],
                                 first=False, last=j == HT - 1)
                last.then_inc(s["out_mm"], 1)

            def up(f):
                def step(kind, img, h):
                    claim(kind, img, f"up{f}", h)
                    pe.wait_ge(s["m_lo"], upto(2 * img + h))
                    part = slice(P * f, P * (f + 1))
                    three(bank(f"up{f}", h), w1h[:, part], w1l[:, part], xh[:, h, :], xl[:, h, :]).then_inc(s["up_mm"], 1)
                return step

            def down(kind, img, h):
                n = 2 * img + h
                claim(kind, img, "down", h)
                bias_first(bank("down", h), BIAS_DOWN)
                pe.wait_ge(s["hid_lo"], upto(n, FT, per=FT))
                for j in range(HT):
                    part = slice(P * j, P * (j + 1))
                    for f in range(FT):
                        last = three(bank("down", h)[:, part], fh[:, f, part], fl[:, f, part], w2h[:, f, :], w2l[:, f, :],
                                     first=False, last=f == FT - 1 and j == HT - 1)
                last.then_inc(s["down_mm"], 1)

            def turn_q(kind, img, h):
                claim(kind, img, "turn_q", h)
                pe.wait_ge(s["qz_made"], upto(2 * img + h))
                dst = bank("turn_q", h)[:, 0:HALF // 2].bitcast(BF16)
                for j in range(HT):
                    last = nc.tensor.transpose(dst[:, P * j:P * (j + 1)], qz[:, h, j, :], identh[:])
                last.then_inc(s["turn_q_mm"], 1)

            def ffn(kind, img, h):
                n = 2 * img + h
                claim(kind, img, "ffn", h)
                pe.wait_ge(s["qt_made"], upto(n))
                for j in range(HT):
                    part = slice(P * j, P * (j + 1))
                    dst = bank("ffn", h)[:, part]
                    mm(dst, t[:, h, j, :], identf[:], is_transpose=True, start=True, stop=False)
                    mm(dst, kh[:], qt[:, h, part], start=False, stop=False)
                    last = mm(dst, kl[:], qt[:, h, part], start=False, stop=True)
                last.then_inc(s["ffn_mm"], 1)

            run(pe, "pe", {"gn1": gn1, "gn2": gn2, "qg": project("qg", QG), "kg": project("kg", KG), "vg": vg, "turn_x": turn_x,
                     "max": row_max, "shift": turn_shift, "st": st, "pv": pv, "turn_in": turn("turn_in", y, 0), "q": q,
                     "k": k, "v": v, "score0": score(0), "score1": score(1), "pv0": pv_win(0), "pv1": pv_win(1),
                     "out": out_proj, "turn_mid": turn("turn_mid", y, 1), "up0": up(0), "up1": up(1), "up2": up(2),
                     "up3": up(3), "down": down, "turn_q": turn_q, "ffn": ffn}, prologue)


SETUP_STEPS = 2 + 12 + 6 + 2 * 10 + 1 + 4 + 2 + 3 + 1 + 5 + 1 + 2


def kernel(**inputs):
    import concourse.bacc as _bacc
    from concourse.bass_utils import run_bass_kernel_spmd as _run

    def arr(name):
        return np.ascontiguousarray(inputs[name])

    qkv_w = arr("L0_conv_qkv_w")
    arrays = {
        "x": arr("x").reshape(IMAGES, C, N),
        "qkv_w_t": np.ascontiguousarray(qkv_w.T), "v_w": np.ascontiguousarray(qkv_w[2 * C:]),
        "proj_w_t": np.ascontiguousarray(arr("L0_conv_proj_w").T),
        "in_w_t": np.ascontiguousarray(arr("L1_attn_in_proj_w").T),
        "out_w_t": np.ascontiguousarray(arr("L1_attn_out_w").T),
        "w1_t": np.ascontiguousarray(arr("L1_attn_w1").T), "w2_t": np.ascontiguousarray(arr("L1_attn_w2").T),
        "kernel": arr("L1_ffn_kernel"), "qkv_b": arr("L0_conv_qkv_b"), "proj_b": arr("L0_conv_proj_b"),
        "gn_w": arr("L0_conv_gn_w"), "gn_b": arr("L0_conv_gn_b"), "in_b": arr("L1_attn_in_proj_b"),
        "out_b": arr("L1_attn_out_b"), "ln1_g": arr("L1_attn_ln1_g"), "ln1_b": arr("L1_attn_ln1_b"),
        "b1": arr("L1_attn_b1"), "b2": arr("L1_attn_b2"), "ln2_g": arr("L1_attn_ln2_g"), "ln2_b": arr("L1_attn_ln2_b"),
        "ffn_b": arr("L1_ffn_bias"), "s_in": arr("L1_ffn_input_scale"), "s_k": arr("L1_ffn_kernel_scale"),
    }
    nc = _bacc.Bacc("TRN2", target_bir_lowering=False, num_devices=1)
    aps = {n: nc.dram_tensor("in_" + n, v.shape, F32, kind="ExternalInput").ap() for n, v in arrays.items()}
    out = nc.dram_tensor("out_y", (IMAGES, C, N), F32, kind="ExternalOutput").ap()
    build(nc, aps, out)
    r = _run(nc, [{"in_" + n: v for n, v in arrays.items()}], core_ids=[0])
    return r.results[0]["out_y"].reshape(IMAGES, C, 32, 32)
```
